# Optimizing a Trainium2 kernel written in Bass

```python
import numpy as np
import jax
import jax.numpy as jnp

def _softmax(x, axis=-1):
    return jax.nn.softmax(x, axis=axis)
def _gelu(x):
    return jax.nn.gelu(x, approximate=True)
def _silu(x):
    return jax.nn.silu(x)
def _sigmoid(x):
    return jax.nn.sigmoid(x)
def _layernorm(x, axis=-1, eps=1e-5):
    m = jnp.mean(x, axis=axis, keepdims=True)
    v = jnp.var(x, axis=axis, keepdims=True)
    return (x - m) / jnp.sqrt(v + eps)
def _scatter_add(tgt, idx, src, axis=0):
    return tgt.at[idx].add(src)
def _segment_sum(src, seg, n):
    return jax.ops.segment_sum(src, seg, n)

kernel_name = 'mk_conv_preact_d4_conv_nchw16_0a193b'

def setup_inputs(seed: int = 0):
    np.random.seed(seed)
    _w = jnp.asarray
    def _rec_inputs():
        import jax
        import jax.numpy as jnp
        _gk = jax.random.key(seed)
        x = -0.0005207 + 1.001 * jax.random.normal(jax.random.fold_in(_gk, 1), (8, 16, 128, 128), jnp.float32)
        return x
    x = _rec_inputs()
    def _L0_conv_setup():
        import jax, jax.numpy as jnp
        import numpy as np
        ENV_D = 16
        N_EMBD = 3 * ENV_D
        N_HEAD = 4
        HEAD_DIM = N_EMBD // N_HEAD
        T = 3
        EPS = 1e-05

        def _ln(x):
            m = jnp.mean(x, axis=-1, keepdims=True)
            v = jnp.var(x, axis=-1, keepdims=True)
            return (x - m) * jax.lax.rsqrt(v + EPS)

        def _fold_to_kernels(in_x):
            B, C, H, W = in_x.shape
            p = jnp.pad(in_x, ((0, 0), (0, 0), (1, 1), (1, 1)), mode='wrap')
            rows = jnp.stack([p[:, :, i:i + H, :] for i in range(3)], axis=2)
            pat = jnp.stack([rows[:, :, :, :, j:j + W] for j in range(3)], axis=4)
            x = jnp.transpose(pat, (0, 3, 5, 4, 1, 2))
            return x.reshape(B * H * W, T, C * 3)

        def _forward(in_x, w_attn, w_attn_proj, w_fc, w_fc_proj, conv_w, conv_b):
            B, C, H, W = in_x.shape
            x = _fold_to_kernels(in_x)
            N = x.shape[0]
            h = _ln(x)
            qkv = h @ w_attn.T
            q, k, v = jnp.split(qkv, 3, axis=-1)

            def heads(t):
                return t.reshape(N, T, N_HEAD, HEAD_DIM).transpose(0, 2, 1, 3)
            q, k, v = (heads(q), heads(k), heads(v))
            att = jnp.einsum('nhtd,nhsd->nhts', q, k) * (1.0 / np.sqrt(HEAD_DIM))
            att = jax.nn.softmax(att, axis=-1)
            y = jnp.einsum('nhts,nhsd->nhtd', att, v)
            y = y.transpose(0, 2, 1, 3).reshape(N, T, N_EMBD)
            x = x + y @ w_attn_proj.T
            h = _ln(x)
            x = x + jax.nn.gelu(h @ w_fc.T, approximate=False) @ w_fc_proj.T
            x = _ln(x)
            x = jnp.sum(x, axis=1).reshape(B, H, W, N_EMBD)
            out = jnp.einsum('bhwc,oc->bohw', x, conv_w) + conv_b[None, :, None, None]
            return out
        key = jax.random.key(seed)
        ks = jax.random.split(key, 7)
        B, H, W = (8, 128, 128)

        def lin(k, shape, fan_in):
            return jax.random.normal(k, shape, jnp.float32) * (1.0 / np.sqrt(fan_in))
        return {'in_x': jax.random.normal(ks[0], (B, ENV_D, H, W), jnp.float32), 'w_attn': lin(ks[1], (3 * N_EMBD, N_EMBD), N_EMBD), 'w_attn_proj': lin(ks[2], (N_EMBD, N_EMBD), N_EMBD), 'w_fc': lin(ks[3], (4 * N_EMBD, N_EMBD), N_EMBD), 'w_fc_proj': lin(ks[4], (N_EMBD, 4 * N_EMBD), 4 * N_EMBD), 'conv_w': lin(ks[5], (ENV_D, N_EMBD), N_EMBD), 'conv_b': jnp.zeros((ENV_D,), jnp.float32)}
    _L0_conv_all = _L0_conv_setup()
    _L0_conv_in = {k: v for k, v in _L0_conv_all.items() if k in ('w_attn', 'w_attn_proj', 'w_fc', 'w_fc_proj', 'conv_w', 'conv_b', )}
    del _L0_conv_all

    def _L1_conv_setup():
        import jax, jax.numpy as jnp
        import numpy as np
        EPS = 1e-05

        def conv1x1(x, W, b):
            return jnp.einsum('oc,bchw->bohw', W, x) + b[None, :, None, None]
        key = jax.random.key(seed)
        ks = jax.random.split(key, 11)
        C = 16
        B, H, W = (8, 512, 512)
        s = 1.0 / np.sqrt(C)
        inp = {'x': jax.random.normal(ks[0], (B, C, H, W), dtype=jnp.float32)}
        names = [('Wc', 'bc'), ('W1', 'b1'), ('W2', 'b2'), ('W3', 'b3'), ('W4', 'b4')]
        for i, (wn, bn) in enumerate(names):
            inp[wn] = jax.random.normal(ks[1 + 2 * i], (C, C), dtype=jnp.float32) * s
            inp[bn] = jax.random.normal(ks[2 + 2 * i], (C,), dtype=jnp.float32) * s
        return inp
    _L1_conv_all = _L1_conv_setup()
    _L1_conv_in = {k: v for k, v in _L1_conv_all.items() if k in ('Wc', 'bc', 'W1', 'b1', 'W2', 'b2', 'W3', 'b3', 'W4', 'b4', )}
    del _L1_conv_all

    def _L2_conv_setup():
        import jax, jax.numpy as jnp
        import numpy as np
        K = 3
        DEG_P = 6
        DEG_Q = 4
        key = jax.random.key(seed)
        k1, k2, k3 = jax.random.split(key, 3)
        B, Cin, Cout, H, W = (4, 16, 16, 64, 64)
        x = jax.random.normal(k1, (B, Cin, H, W), dtype=jnp.float32)
        A = jax.random.normal(k2, (Cout, Cin, K * K, DEG_P), dtype=jnp.float32) * 0.1
        Bc = jax.random.normal(k3, (Cout, Cin, K * K, DEG_Q), dtype=jnp.float32) * 0.1
        return {'x': x, 'A': A, 'Bc': Bc}
    _L2_conv_all = _L2_conv_setup()
    _L2_conv_in = {k: v for k, v in _L2_conv_all.items() if k in ('A', 'Bc', )}
    del _L2_conv_all

    def _L3_conv_setup():
        import jax, jax.numpy as jnp
        import numpy as np
        GRID_SIZE = 5
        SPLINE_ORDER = 3
        KSIZE = 3
        STRIDE = 1
        PAD = 1
        NBASES = GRID_SIZE + SPLINE_ORDER

        def _grid():
            h = 2.0 / GRID_SIZE
            return jnp.arange(-SPLINE_ORDER, GRID_SIZE + SPLINE_ORDER + 1, dtype=jnp.float32) * h - 1.0

        def _b_splines(x, grid):
            x = x[..., None]
            bases = ((x >= grid[:-1]) & (x < grid[1:])).astype(x.dtype)
            for k in range(1, SPLINE_ORDER + 1):
                left = (x - grid[:-(k + 1)]) / (grid[k:-1] - grid[:-(k + 1)]) * bases[..., :-1]
                right = (grid[k + 1:] - x) / (grid[k + 1:] - grid[1:-k]) * bases[..., 1:]
                bases = left + right
            return bases

        def _extract_patches(x, k, stride, padding):
            if padding > 0:
                x = jnp.pad(x, ((0, 0), (0, 0), (padding, padding), (padding, padding)))
            B, C, H, W = x.shape
            oh = (H - k) // stride + 1
            ow = (W - k) // stride + 1
            cols = [x[:, :, dh:dh + (oh - 1) * stride + 1:stride, dw:dw + (ow - 1) * stride + 1:stride] for dh in range(k) for dw in range(k)]
            return jnp.stack(cols, axis=-1)
        key = jax.random.key(seed)
        ks = jax.random.split(key, 5)
        B, Cin, Cout, H, W = (4, 16, 16, 128, 128)
        k2 = KSIZE * KSIZE
        x = jax.random.normal(ks[0], (B, Cin, H, W), dtype=jnp.float32)
        base_weight = jax.random.normal(ks[1], (Cout, Cin, k2, k2), dtype=jnp.float32) * (1.0 / np.sqrt(k2))
        spline_weight = jax.random.normal(ks[2], (Cout, Cin, k2, k2, NBASES), dtype=jnp.float32) * 0.1
        spline_scaler = jax.random.normal(ks[3], (Cout, Cin, k2, k2), dtype=jnp.float32) * (1.0 / np.sqrt(k2))
        bias_weight = jax.random.normal(ks[4], (Cout,), dtype=jnp.float32)
        return {'x': x, 'base_weight': base_weight, 'spline_weight': spline_weight, 'spline_scaler': spline_scaler, 'bias_weight': bias_weight}
    _L3_conv_all = _L3_conv_setup()
    _L3_conv_in = {k: v for k, v in _L3_conv_all.items() if k in ('base_weight', 'spline_weight', 'spline_scaler', 'bias_weight', )}
    del _L3_conv_all

    return {
        "x": x,
        "L0_conv_w_attn": _L0_conv_in["w_attn"],
        "L0_conv_w_attn_proj": _L0_conv_in["w_attn_proj"],
        "L0_conv_w_fc": _L0_conv_in["w_fc"],
        "L0_conv_w_fc_proj": _L0_conv_in["w_fc_proj"],
        "L0_conv_conv_w": _L0_conv_in["conv_w"],
        "L0_conv_conv_b": _L0_conv_in["conv_b"],
        "L1_conv_Wc": _L1_conv_in["Wc"],
        "L1_conv_bc": _L1_conv_in["bc"],
        "L1_conv_W1": _L1_conv_in["W1"],
        "L1_conv_b1": _L1_conv_in["b1"],
        "L1_conv_W2": _L1_conv_in["W2"],
        "L1_conv_b2": _L1_conv_in["b2"],
        "L1_conv_W3": _L1_conv_in["W3"],
        "L1_conv_b3": _L1_conv_in["b3"],
        "L1_conv_W4": _L1_conv_in["W4"],
        "L1_conv_b4": _L1_conv_in["b4"],
        "L2_conv_A": _L2_conv_in["A"],
        "L2_conv_Bc": _L2_conv_in["Bc"],
        "L3_conv_base_weight": _L3_conv_in["base_weight"],
        "L3_conv_spline_weight": _L3_conv_in["spline_weight"],
        "L3_conv_spline_scaler": _L3_conv_in["spline_scaler"],
        "L3_conv_bias_weight": _L3_conv_in["bias_weight"],
    }

def reference(x, L0_conv_w_attn, L0_conv_w_attn_proj, L0_conv_w_fc, L0_conv_w_fc_proj, L0_conv_conv_w, L0_conv_conv_b, L1_conv_Wc, L1_conv_bc, L1_conv_W1, L1_conv_b1, L1_conv_W2, L1_conv_b2, L1_conv_W3, L1_conv_b3, L1_conv_W4, L1_conv_b4, L2_conv_A, L2_conv_Bc, L3_conv_base_weight, L3_conv_spline_weight, L3_conv_spline_scaler, L3_conv_bias_weight):
    import jax
    import jax.numpy as jnp
    def _L0_conv_ref(in_x, w_attn, w_attn_proj, w_fc, w_fc_proj, conv_w, conv_b):
        import jax, jax.numpy as jnp
        import numpy as np
        ENV_D = 16
        N_EMBD = 3 * ENV_D
        N_HEAD = 4
        HEAD_DIM = N_EMBD // N_HEAD
        T = 3
        EPS = 1e-05

        def _ln(x):
            m = jnp.mean(x, axis=-1, keepdims=True)
            v = jnp.var(x, axis=-1, keepdims=True)
            return (x - m) * jax.lax.rsqrt(v + EPS)

        def _fold_to_kernels(in_x):
            B, C, H, W = in_x.shape
            p = jnp.pad(in_x, ((0, 0), (0, 0), (1, 1), (1, 1)), mode='wrap')
            rows = jnp.stack([p[:, :, i:i + H, :] for i in range(3)], axis=2)
            pat = jnp.stack([rows[:, :, :, :, j:j + W] for j in range(3)], axis=4)
            x = jnp.transpose(pat, (0, 3, 5, 4, 1, 2))
            return x.reshape(B * H * W, T, C * 3)

        def _forward(in_x, w_attn, w_attn_proj, w_fc, w_fc_proj, conv_w, conv_b):
            B, C, H, W = in_x.shape
            x = _fold_to_kernels(in_x)
            N = x.shape[0]
            h = _ln(x)
            qkv = h @ w_attn.T
            q, k, v = jnp.split(qkv, 3, axis=-1)

            def heads(t):
                return t.reshape(N, T, N_HEAD, HEAD_DIM).transpose(0, 2, 1, 3)
            q, k, v = (heads(q), heads(k), heads(v))
            att = jnp.einsum('nhtd,nhsd->nhts', q, k) * (1.0 / np.sqrt(HEAD_DIM))
            att = jax.nn.softmax(att, axis=-1)
            y = jnp.einsum('nhts,nhsd->nhtd', att, v)
            y = y.transpose(0, 2, 1, 3).reshape(N, T, N_EMBD)
            x = x + y @ w_attn_proj.T
            h = _ln(x)
            x = x + jax.nn.gelu(h @ w_fc.T, approximate=False) @ w_fc_proj.T
            x = _ln(x)
            x = jnp.sum(x, axis=1).reshape(B, H, W, N_EMBD)
            out = jnp.einsum('bhwc,oc->bohw', x, conv_w) + conv_b[None, :, None, None]
            return out
        return _forward(in_x, w_attn, w_attn_proj, w_fc, w_fc_proj, conv_w, conv_b)

    def _L1_conv_ref(x, Wc, bc, W1, b1, W2, b2, W3, b3, W4, b4):
        import jax, jax.numpy as jnp
        import numpy as np
        EPS = 1e-05

        def conv1x1(x, W, b):
            return jnp.einsum('oc,bchw->bohw', W, x) + b[None, :, None, None]
        out1 = jnp.mean(x, axis=(2, 3), keepdims=True)
        out3 = jnp.max(x, axis=(2, 3), keepdims=True)
        out2 = conv1x1(x, Wc, bc)
        out4 = conv1x1(x, W1, b1)
        wh = conv1x1(out2 / (out1 + EPS), W2, b2)
        wh_weight = jax.nn.sigmoid(jnp.tanh(wh))
        gray = conv1x1(out4 / (out3 + EPS), W3, b3)
        gray_weight = jax.nn.sigmoid(jnp.tanh(gray))
        out = conv1x1(x * (1.0 + wh_weight + gray_weight), W4, b4)
        return out

    def _L2_conv_ref(x, A, Bc):
        import jax, jax.numpy as jnp
        import numpy as np
        K = 3
        DEG_P = 6
        DEG_Q = 4
        B, C, H, W = x.shape
        pad = (K - 1) // 2
        xp = jnp.pad(x, ((0, 0), (0, 0), (pad, pad), (pad, pad)))
        wins = jnp.stack([xp[:, :, i:i + H, j:j + W] for i in range(K) for j in range(K)])
        pw = wins[..., None] ** jnp.arange(DEG_P, dtype=x.dtype)
        P = jnp.einsum('pbchwi,fcpi->fpbchw', pw, A)
        Q = 1.0 + jnp.abs(jnp.einsum('pbchwi,fcpi->fpbchw', pw[..., 1:1 + DEG_Q], Bc))
        out = jnp.sum(P / Q, axis=(1, 3))
        return jnp.transpose(out, (1, 0, 2, 3))

    def _L3_conv_ref(x, base_weight, spline_weight, spline_scaler, bias_weight):
        import jax, jax.numpy as jnp
        import numpy as np
        GRID_SIZE = 5
        SPLINE_ORDER = 3
        KSIZE = 3
        STRIDE = 1
        PAD = 1
        NBASES = GRID_SIZE + SPLINE_ORDER

        def _grid():
            h = 2.0 / GRID_SIZE
            return jnp.arange(-SPLINE_ORDER, GRID_SIZE + SPLINE_ORDER + 1, dtype=jnp.float32) * h - 1.0

        def _b_splines(x, grid):
            x = x[..., None]
            bases = ((x >= grid[:-1]) & (x < grid[1:])).astype(x.dtype)
            for k in range(1, SPLINE_ORDER + 1):
                left = (x - grid[:-(k + 1)]) / (grid[k:-1] - grid[:-(k + 1)]) * bases[..., :-1]
                right = (grid[k + 1:] - x) / (grid[k + 1:] - grid[1:-k]) * bases[..., 1:]
                bases = left + right
            return bases

        def _extract_patches(x, k, stride, padding):
            if padding > 0:
                x = jnp.pad(x, ((0, 0), (0, 0), (padding, padding), (padding, padding)))
            B, C, H, W = x.shape
            oh = (H - k) // stride + 1
            ow = (W - k) // stride + 1
            cols = [x[:, :, dh:dh + (oh - 1) * stride + 1:stride, dw:dw + (ow - 1) * stride + 1:stride] for dh in range(k) for dw in range(k)]
            return jnp.stack(cols, axis=-1)
        patches = _extract_patches(x, KSIZE, STRIDE, PAD)
        grid = _grid()
        bspl = _b_splines(patches, grid)
        base_w = base_weight.sum(axis=2)
        spl_w = (spline_weight * spline_scaler[..., None]).sum(axis=2)
        out = jnp.einsum('bjhwn,ijn->bihw', jax.nn.silu(patches), base_w)
        out = out + jnp.einsum('bjhwns,ijns->bihw', bspl, spl_w)
        out = out + bias_weight[None, :, None, None]
        return out

    def _gn(v, G=8, eps=1e-5):
        B_, C_, H_, W_ = v.shape
        g = v.reshape(B_, G, C_ // G, H_, W_)
        m = jnp.mean(g, axis=(2, 3, 4), keepdims=True)
        s = jnp.var(g, axis=(2, 3, 4), keepdims=True)
        return ((g - m) / jnp.sqrt(s + eps)).reshape(v.shape)

    def _ln_c(v, eps=1e-6):
        m = jnp.mean(v, axis=1, keepdims=True)
        s = jnp.var(v, axis=1, keepdims=True)
        return (v - m) / jnp.sqrt(s + eps)

    def _ln_t(v, eps=1e-5):
        m = jnp.mean(v, axis=-1, keepdims=True)
        s = jnp.var(v, axis=-1, keepdims=True)
        return (v - m) / jnp.sqrt(s + eps)

    def _to_tokens(v):
        B_, C_, H_, W_ = v.shape
        return v.reshape(B_, C_, H_ * W_).transpose(0, 2, 1)
    def _from_tokens(t, like):
        B_, C_, H_, W_ = like.shape
        return t.transpose(0, 2, 1).reshape(B_, C_, H_, W_)

    x = x + _L0_conv_ref(_gn(x), L0_conv_w_attn, L0_conv_w_attn_proj, L0_conv_w_fc, L0_conv_w_fc_proj, L0_conv_conv_w, L0_conv_conv_b)
    x = x + _L1_conv_ref(_gn(x), L1_conv_Wc, L1_conv_bc, L1_conv_W1, L1_conv_b1, L1_conv_W2, L1_conv_b2, L1_conv_W3, L1_conv_b3, L1_conv_W4, L1_conv_b4)
    x = x + _L2_conv_ref(_gn(x), L2_conv_A, L2_conv_Bc)
    x = x + _L3_conv_ref(_gn(x), L3_conv_base_weight, L3_conv_spline_weight, L3_conv_spline_scaler, L3_conv_bias_weight)
    return x


_drawn_inputs = setup_inputs


def setup_inputs(seed=0):
    import zlib

    import numpy as np

    out = dict(_drawn_inputs(seed))
    spreads = {'L0_conv_conv_b': (0.0, 0.1)}
    factors = {'L1_conv_b1': 7.184, 'L1_conv_b2': 8.0}
    for name, (base, spread) in spreads.items():
        noise = np.random.default_rng([zlib.crc32(name.encode()), seed]).standard_normal(out[name].shape)
        drawn = base * np.exp(spread * noise) if base else spread * noise
        out[name] = jnp.asarray(drawn.astype(out[name].dtype))
    for name, factor in factors.items():
        out[name] = (out[name] * factor).astype(out[name].dtype)
    return out
```

```python
import concourse.bass as bass
from concourse import mybir
from contextlib import ExitStack

F32 = mybir.dt.float32
BF16 = mybir.dt.bfloat16
I32 = mybir.dt.int32
ALU = mybir.AluOpType
ACT = mybir.ActivationFunctionType
AX = mybir.AxisListType

P = 128
NB, C, H, W = 8, 16, 128, 128
HW = H * W
GN_EPS = 1e-5

PW = W + 1
SUB = 509
IMG = 33 * SUB
LINE = NB * IMG
NSUB = 4
SUP = NSUB * SUB
NSUP = LINE // SUP
SLOTS = 3
assert IMG >= (H + 2) * PW + 1 and NSUP * SUP == LINE and NSUP % SLOTS == 0
OFFS = [dy * PW + dx for dy in (-1, 0, 1) for dx in (-1, 0, 1)]
CENTER = 4
AROUND = [n for n in range(9) if n != CENTER]
MARGIN = 256
assert MARGIN >= max(OFFS)

X_PARTS = [0, 0, 0, 1, 1, 2]
A_PARTS = [0, 1, 2, 0, 1, 0]
DEG = 5
CG = 4
NCG = C // CG
KROWS = len(X_PARTS) * CG * DEG + 3
assert KROWS <= P


def image_rows(t):
    return t[:, PW:PW + H * PW].rearrange("p (h w) -> p h w", w=PW)[:, :, 1:1 + W]


class Chain:

    def __init__(self, engine, sem):
        self.engine, self.sem, self.n = engine, sem, 0

    def __call__(self, instruction):
        self.n += 1
        instruction.then_inc(self.sem, 1)
        self.engine.wait_ge(self.sem, self.n)


class Norm:

    CHUNKS = 32

    def __init__(self, nc, ctx, tag):
        def sb(name, shape):
            return ctx.enter_context(nc.sbuf_tensor(f"{tag}_{name}", shape, F32))

        self.nc = nc
        self.stats = sb("stats", [P, self.CHUNKS, 6])
        self.own = sb("own", [P, 2])
        self.dev = sb("dev", [P, 2])
        self.spread = sb("spread", [P, 1])
        self.mean = sb("mean", [P, 1])
        self.std = sb("std", [P, 1])
        self.rstd = sb("rstd", [P, 1])
        self.shift = sb("shift", [P, 1])
        self.eps = sb("eps", [P, 1])
        self.pair = sb("pair", [P, P])
        self.sums = ctx.enter_context(nc.psum_tensor(f"{tag}_sums", [P, 2], F32))
        self.pair_in = ctx.enter_context(nc.semaphore(f"{tag}_pair_in"))
        self.own_ready = ctx.enter_context(nc.semaphore(f"{tag}_own_ready"))
        self.mean_ready = ctx.enter_context(nc.semaphore(f"{tag}_mean_ready"))
        self.spread_ready = ctx.enter_context(nc.semaphore(f"{tag}_spread_ready"))
        self.var_ready = ctx.enter_context(nc.semaphore(f"{tag}_var_ready"))
        self.std_ready = ctx.enter_context(nc.semaphore(f"{tag}_std_ready"))

    def sync_part(self, sp, pair_dram):
        sp.dma_start(self.pair[:], pair_dram).then_inc(self.pair_in, 16)

    def vector_part(self, dve, link, x, chunk_in):
        v = self.nc.vector
        v.memset(self.eps[:], GN_EPS)
        n = HW // self.CHUNKS
        for k in range(self.CHUNKS):
            chunk_in(dve, k)
            last = v.bn_stats(self.stats[:, k, :], x(k, n))
        link(last)
        link(v.bn_aggr(self.own[:], self.stats[:].rearrange("p k s -> p (k s)")))
        link(v.tensor_copy(self.spread[:], self.own[:, 0:1]))
        v.tensor_copy(self.mean[:], self.own[:, 0:1]).then_inc(self.own_ready, 1)
        dve.wait_ge(self.mean_ready, 1)
        link(v.tensor_copy(self.mean[:], self.sums[:, 0:1]))
        link(v.tensor_tensor(self.dev[:, 0:1], self.own[:, 0:1], self.mean[:], ALU.subtract))
        link(v.tensor_tensor(self.dev[:, 1:2], self.dev[:, 0:1], self.dev[:, 0:1], ALU.mult))
        v.tensor_tensor(self.spread[:], self.own[:, 1:2], self.dev[:, 1:2],
                        ALU.add).then_inc(self.spread_ready, 1)
        dve.wait_ge(self.std_ready, 1)
        link(v.reciprocal(self.rstd[:], self.std[:]))
        link(v.scalar_tensor_tensor(self.shift[:], self.mean[:], -1.0, self.rstd[:], ALU.mult, ALU.mult))

    def tensor_part(self, pe):
        t = self.nc.tensor
        pe.wait_ge(self.pair_in, 16)
        pe.wait_ge(self.own_ready, 1)
        t.matmul(self.sums[:, 0:1], self.pair[:], self.own[:, 0:1], start=True, stop=True).then_inc(self.mean_ready, 1)
        pe.wait_ge(self.spread_ready, 1)
        t.matmul(self.sums[:, 1:2], self.pair[:], self.spread[:], start=True, stop=True).then_inc(self.var_ready, 1)

    def scalar_part(self, act):
        act.wait_ge(self.var_ready, 1)
        self.nc.scalar.activation(self.std[:], self.sums[:, 1:2], ACT.Sqrt, bias=self.eps[:]).then_inc(self.std_ready, 1)


EMB = 3 * C
SETS = 2
F2 = SETS * EMB
HEADS, HEAD = 4, 12
SH = SETS * HEADS
CW = 8
TW = CW + 2
NCHUNK = W // CW
NPAIR = NB // SETS
HID = 4 * EMB
LN_EPS = 1e-5
T_GROUPS = {"norm1": 4, "mix": 6, "norm2": 6, "norm3": 2}
T_WIDTHS = (3, 3, 2, 2)
C_GROUPS = {"proj": 6, "mlp": 6, "conv": 2}


class Plan:

    def __init__(self, pair, t, attn, mlp):
        self.attn, self.mlp, self.pair = attn, mlp, pair
        self.chunk = pair * NCHUNK + t
        self.behind = pair * NCHUNK + t - 1
        order_t = ("norm1", "norm2", "mix", "norm3")
        order_c = ("mlp", "proj", "conv")
        at, ac = ("norm1", "mix"), ("proj",)

        def half(names, groups, first):
            return sum(groups[n] for n in names if (n in first))

        ta, tb = half(order_t, T_GROUPS, at), sum(T_GROUPS.values()) - half(order_t, T_GROUPS, at)
        ca, cb = half(order_c, C_GROUPS, ac), sum(C_GROUPS.values()) - half(order_c, C_GROUPS, ac)
        first = not mlp
        self.t_base = pair * (NCHUNK * (ta + tb)) + (0 if first else t * (ta + tb) - tb)
        self.c_base = pair * (NCHUNK * (ca + cb)) + (0 if first else t * (ca + cb) - cb)
        self.t, self.c, nt, ncn = {}, {}, 0, 0
        for n in order_t:
            if attn if n in at else mlp:
                self.t[n], nt = nt, nt + T_GROUPS[n]
        for n in order_c:
            if attn if n in ac else mlp:
                self.c[n], ncn = ncn, ncn + C_GROUPS[n]


def steps(engine, body):
    with engine.Fori(0, NPAIR) as pair:
        body(Plan(pair, 0, True, False))
        with engine.Fori(1, NCHUNK) as t:
            body(Plan(pair, t, True, True), t)
        body(Plan(pair, NCHUNK, False, True))


def norm0(nc, x, pair, g0):
    ROWS = 32
    with ExitStack() as ctx:
        def sb(name, shape, dt=F32):
            return ctx.enter_context(nc.sbuf_tensor(name, shape, dt))

        def sem(name):
            return ctx.enter_context(nc.semaphore(name))

        norm = Norm(nc, ctx, "n0")
        X = sb("n0_x", [P, HW])
        G = sb("n0_g", [P, H, W + 2])
        x_in = [sem(f"n0_x_in{k}") for k in range(8)]
        chain, ready, stored = sem("n0_chain"), sem("n0_ready"), sem("n0_stored")
        with nc.Block() as block:
            @block.sync
            def _(sp):
                for k in range(8):
                    sp.dma_start(X[:, k * HW // 8:(k + 1) * HW // 8], x[:, k * HW // 8:(k + 1) * HW // 8]).then_inc(x_in[k], 16)
                norm.sync_part(sp, pair)
                for k in range(H // ROWS):
                    sp.wait_ge(ready, 3 * (k + 1))
                    sp.dma_start(g0[:, k * ROWS:(k + 1) * ROWS, :], G[:, k * ROWS:(k + 1) * ROWS, :]).then_inc(stored, 16)
                sp.wait_ge(stored, H // ROWS * 16)

            @block.vector
            def _(dve):
                v = nc.vector
                link = Chain(dve, chain)
                norm.vector_part(dve, link, lambda k, n: X[:, k * n:(k + 1) * n],
                                 lambda e, k: e.wait_ge(x_in[k // 4], 16))
                x3 = X[:].rearrange("p (h w) -> p h w", w=W)
                for k in range(H // ROWS):
                    r = slice(k * ROWS, (k + 1) * ROWS)
                    for to, of in ((slice(1, W + 1), slice(0, W)), (slice(0, 1), slice(W - 1, W)), (slice(W + 1, W + 2), slice(0, 1))):
                        v.tensor_scalar(G[:, r, to], x3[:, r, of], norm.rstd[:], norm.shift[:], ALU.mult, ALU.add).then_inc(ready, 1)

            @block.tensor
            def _(pe):
                norm.tensor_part(pe)

            @block.scalar
            def _(act):
                norm.scalar_part(act)


def layer0(nc, io, g0, x1):
    with ExitStack() as ctx:
        def sb(name, shape, dt=F32):
            return ctx.enter_context(nc.sbuf_tensor(name, shape, dt))

        def ps(name, shape):
            return ctx.enter_context(nc.psum_tensor(name, shape, F32))

        def sem(name):
            return ctx.enter_context(nc.semaphore(name))

        ident = sb("a_ident", [P, P])
        wqkv = sb("a_wqkv", [F2, 3 * F2])
        wproj = sb("a_wproj", [F2, F2])
        wfc = sb("a_wfc", [F2, SETS * HID])
        wfp = sb("a_wfp", [P, 3, F2])
        wconv = sb("a_wconv", [F2, SETS * C])
        cbias = sb("a_cbias", [P, SETS * C])
        raw = sb("a_raw", [F2, F2 + SETS * HID + F2])
        eps = sb("a_eps", [P, 1])
        TB = sb("a_tb", [P, F2, W + 2])
        XB = sb("a_xb", [P, SETS * C, W])
        Tc = sb("a_tc", [P, TW, F2])
        hA = sb("a_ha", [P, TW, F2])
        hAT = sb("a_hat", [F2, TW, P])
        QKV = sb("a_qkv", [P, TW, 3 * F2])
        PR = sb("a_pr", [P, 9, CW * F2])
        Sc = sb("a_sc", [P, 5, TW, SH])
        At = sb("a_at", [P, 3, 3, CW * SH])
        yT = sb("a_yt", [F2, 3, CW, P])
        x1c = sb("a_x1c", [P, 3, CW, F2])
        hB = sb("a_hb", [P, 3, CW, F2])
        hBT = sb("a_hbt", [F2, 3 * CW, P])
        G = sb("a_g", [P, 2, 3, 512])
        x2c = sb("a_x2c", [P, 3, CW, F2])
        zs = sb("a_zs", [P, CW, F2])
        zT = sb("a_zt", [F2, CW, P])
        st = sb("a_st", [P, 8, 3 * CW * SETS])
        sm = sb("a_sm", [P, 3, 3 * CW * SH])
        tps = ps("a_tps", [P, 2, 512])
        qps = ps("a_qps", [P, 2, 512])
        fps = ps("a_fps", [P, 2, 512])
        cps = ps("a_cps", [P, 2, 512])

        w_in, cent_made, w_ready = sem("a_w_in"), sem("a_cent_made"), sem("a_w_ready")
        tb_in, xb_in, xb_ready, stored = sem("a_tb_in"), sem("a_xb_in"), sem("a_xb_ready"), sem("a_stored")
        n1 = sem("a_n1")
        n1_sq, n1_r = sem("a_n1_sq"), sem("a_n1_r")
        sc_v, sc_p = sem("a_sc_v"), sem("a_sc_p")
        soft, soft_exp = sem("a_soft"), sem("a_soft_exp")
        val_v, val_p = sem("a_val_v"), sem("a_val_p")
        n2, n2_sq, n2_r = sem("a_n2"), sem("a_n2_sq"), sem("a_n2_r")
        n3, n3_sq, n3_r = sem("a_n3"), sem("a_n3_sq"), sem("a_n3_r")
        t_made, t_read = sem("a_t_made"), sem("a_t_read")
        q_made, q_read = sem("a_q_made"), sem("a_q_read")
        f_made, f_read = sem("a_f_made"), sem("a_f_read")
        c_made, c_read = sem("a_c_made"), sem("a_c_read")
        CPP = NCHUNK * sum(C_GROUPS.values())

        with nc.Block() as block:
            def x1v(pair, s):
                n = pair * SETS + s
                return x1[n * C:(n + 1) * C].rearrange("c (h w) -> h c w", w=W)

            @block.sync
            def _(sp):
                for t, src in ((ident, io["ident"]), (wqkv, io["w0_qkv"]), (wfc, io["w0_fc"]), (wconv, io["w0_conv"]),
                               (cbias, io["w0_bias"])):
                    sp.dma_start(t[:], src).then_inc(w_in, 16)
                at = 0
                for src, n in ((io["w0_proj"], F2), (io["w0_fc_proj"], SETS * HID), (io["w0_center"], F2)):
                    sp.dma_start(raw[:, at:at + n], src).then_inc(w_in, 16)
                    at += n
                for pair in range(NPAIR):
                    if pair:
                        sp.wait_ge(n1, pair * NCHUNK * 5)
                    for s in range(SETS):
                        rows = g0[(pair * SETS + s) * C:(pair * SETS + s + 1) * C]
                        for i in range(3):
                            to = TB[:, s * EMB + i * C:s * EMB + (i + 1) * C, :]
                            lo, hi = max(0, 1 - i), min(H, H + 1 - i)
                            sp.dma_start(to[lo:hi], rows[:, lo + i - 1:hi + i - 1, :].rearrange("c h w -> h c w")).then_inc(tb_in, 16)
                            if i != 1:
                                edge, of = (0, H - 1) if i == 0 else (H - 1, 0)
                                sp.dma_start(to[edge:edge + 1], rows[:, of:of + 1, :].rearrange("c h w -> h c w")).then_inc(tb_in, 16)
                    if pair:
                        sp.wait_ge(c_read, pair * CPP + 2)
                        for s in range(SETS):
                            sp.dma_start(x1v(pair - 1, s), XB[:, s * C:(s + 1) * C, :]).then_inc(stored, 16)
                        sp.wait_ge(stored, pair * SETS * 16)
                    for s in range(SETS):
                        sp.dma_start(XB[:, s * C:(s + 1) * C, :],
                                     io["x"][pair * SETS + s].rearrange("c h w -> h c w")).then_inc(xb_in, 16)
                sp.wait_ge(c_read, NPAIR * CPP + 2)
                for s in range(SETS):
                    sp.dma_start(x1v(NPAIR - 1, s), XB[:, s * C:(s + 1) * C, :]).then_inc(stored, 16)
                sp.wait_ge(stored, NPAIR * SETS * 16)

            @block.tensor
            def _(pe):
                t_ = nc.tensor
                pe.wait_ge(w_in, 8 * 16)
                center = raw[:, F2 + SETS * HID:]
                t_.matmul(cps[0:F2, 0, 0:F2], raw[:, 0:F2], center, start=True, stop=True)
                for m in range(3):
                    last = t_.matmul(cps[:, 1, m * F2:(m + 1) * F2], raw[:, F2 + m * P:F2 + (m + 1) * P], center,
                                     start=True, stop=True)
                last.then_inc(cent_made, 1)
                pe.wait_ge(w_ready, 2)

                def transposes(src, first, n, base, k):
                    pe.wait_ge(t_read, base + k + 1)
                    for j in range(n):
                        last = t_.matmul(tps[0:F2, k % 2, j * P:(j + 1) * P], src[:, first + j, :], ident[:],
                                         start=True, stop=True)
                    last.then_inc(t_made, 1)

                def body(p, t=None):
                    if p.attn:
                        k = p.chunk
                        pe.wait_ge(n1, k * 5 + 5)
                        at = 0
                        for g, n in enumerate(T_WIDTHS):
                            transposes(hA, at, n, p.t_base, p.t["norm1"] + g)
                            at += n
                        at = 0
                        for g, n in enumerate(T_WIDTHS):
                            pe.wait_ge(t_read, p.t_base + p.t["norm1"] + g + 1 + 2)
                            for w in range(at, at + n):
                                pe.wait_ge(q_read, k * TW + w + 1)
                                t_.matmul(qps[:, w % 2, 0:3 * F2], hAT[:, w, :], wqkv[:], start=True, stop=True).then_inc(q_made, 1)
                            at += n
                    if p.mlp:
                        kb = p.behind
                        pe.wait_ge(n2, kb * 2 + 2)
                        for g in range(6):
                            transposes(hB[:].rearrange("p t w f -> p (t w) f"), g * 4, 4, p.t_base, p.t["norm2"] + g)
                        hidden(p, kb, 0)
                        for g in range(6):
                            if g < 5:
                                hidden(p, kb, g + 1)
                            pe.wait_ge(f_read, kb * 18 + g * 3 + 3 + 2)
                            c = p.c["mlp"] + g
                            pe.wait_ge(c_read, p.c_base + c + 1)
                            for j in range(4):
                                for m, lo, hi in ((1, 0, F2), (0, 0, EMB), (2, EMB, F2)):
                                    last = t_.matmul(cps[:, c % 2, j * F2 + lo:j * F2 + hi], G[:, g % 2, m, j * P:(j + 1) * P],
                                                     wfp[:, m, lo:hi], start=m == 1, stop=m == 2, skip_group_check=True)
                            last.then_inc(c_made, 1)
                    if p.attn:
                        k = p.chunk
                        for d in range(3):
                            pe.wait_ge(val_p, k * 6 + 2 * d + 2)
                            for half in range(2):
                                transposes(PR[:, 3 * d, :].rearrange("p (w f) -> p w f", f=F2), half * 4, 4,
                                           p.t_base, p.t["mix"] + 2 * d + half)
                        for g in range(6):
                            pe.wait_ge(t_read, p.t_base + p.t["mix"] + g + 1 + 2)
                            c = p.c["proj"] + g
                            pe.wait_ge(c_read, p.c_base + c + 1)
                            for j in range(4):
                                last = t_.matmul(cps[:, c % 2, j * F2:(j + 1) * F2], yT[:, g // 2, (g % 2) * 4 + j, :], wproj[:],
                                                 start=True, stop=True)
                            last.then_inc(c_made, 1)
                    if p.mlp:
                        pe.wait_ge(n3, kb * 4 + 4)
                        for g in range(2):
                            transposes(zs, g * 4, 4, p.t_base, p.t["norm3"] + g)
                        for g in range(2):
                            pe.wait_ge(t_read, p.t_base + p.t["norm3"] + g + 1 + 2)
                            c = p.c["conv"] + g
                            pe.wait_ge(c_read, p.c_base + c + 1)
                            for j in range(4):
                                last = t_.matmul(cps[:, c % 2, j * 32:(j + 1) * 32], zT[:, g * 4 + j, :], wconv[:],
                                                 start=True, stop=True)
                            last.then_inc(c_made, 1)

                def hidden(p, kb, g):
                    pe.wait_ge(t_read, p.t_base + p.t["norm2"] + g + 1 + 2)
                    for m in range(3):
                        n = g * 3 + m
                        pe.wait_ge(f_read, kb * 18 + n + 1)
                        t_.matmul(fps[:, n % 2, :], wfc[:, m * P:(m + 1) * P],
                                  hBT[:, g * 4:(g + 1) * 4, :].rearrange("f w h -> f (w h)"), start=True, stop=True).then_inc(f_made, 1)

                steps(pe, body)

            def scratch(d):
                n = TW * F2
                return PR[:].rearrange("p k n -> p (k n)")[:, (d + 2) * n:(d + 3) * n].rearrange("p (w f) -> p w f", f=F2)

            def query_key(engine, d):
                lo, m = max(0, -d), TW - abs(d)
                return engine.tensor_tensor(scratch(d)[:, 0:m, :], QKV[:, lo:lo + m, 0:F2],
                                            QKV[:, lo + d:lo + d + m, F2:2 * F2], ALU.mult)

            @block.vector
            def _(dve):
                v = nc.vector
                dve.sem_inc(c_read, 2)
                v.memset(eps[:], LN_EPS).then_inc(w_ready, 1)
                dve.wait_ge(cent_made, 1)
                v.tensor_copy(wproj[:], cps[0:F2, 0, 0:F2])
                v.tensor_copy(wfp[:].rearrange("p m f -> p (m f)"), cps[:, 1, 0:3 * F2]).then_inc(w_ready, 1)
                dve.wait_ge(w_ready, 2)

                def own(sem_, base, instruction, i):
                    instruction.then_inc(sem_, 1)
                    dve.wait_ge(sem_, base + i)

                def norm_tokens(p, t):
                    k = p.chunk
                    b = k * 5
                    w0 = 0 if t is None else t * CW
                    tok = TB[:, :, bass.ds(w0, TW)]
                    total, mean, var, r = (st[:, n, 0:TW * SETS] for n in range(4))
                    dve.wait_ge(q_read, k * TW + 2)
                    own(n1, b, v.tensor_reduce(total.rearrange("p (w s) -> p w s", s=SETS),
                                               tok.rearrange("p (s f) w -> p w s f", s=SETS), AX.X, ALU.add), 1)
                    own(n1, b, v.tensor_scalar(mean, total, 1.0 / EMB, None, ALU.mult), 2)
                    own(n1, b, v.tensor_tensor(Tc[:].rearrange("p w (s f) -> p w s f", s=SETS),
                                               tok.rearrange("p (s f) w -> p w s f", s=SETS),
                                               mean.rearrange("p (w s) -> p w s", s=SETS).unsqueeze(3).broadcast_to([P, TW, SETS, EMB]),
                                               ALU.subtract), 3)
                    dve.wait_ge(n1_sq, k + 1)
                    own(n1, b, v.tensor_reduce(var, hA[:].rearrange("p w (s f) -> p (w s) f", s=SETS), AX.X, ALU.add), 4)
                    dve.wait_ge(n1_r, k * 2 + 2)
                    own(n1, b, v.tensor_tensor(hA[:].rearrange("p w (s f) -> p (w s) f", s=SETS),
                                               Tc[:].rearrange("p w (s f) -> p (w s) f", s=SETS),
                                               r.unsqueeze(2).broadcast_to([P, TW * SETS, EMB]), ALU.mult), 5)

                def norm_residual(p):
                    kb = p.behind
                    var, r = st[:, 4, :], st[:, 5, :]
                    dve.wait_ge(n2_sq, kb + 1)
                    h = hB[:].rearrange("p t w (s f) -> p (t w s) f", s=SETS)
                    own(n2, kb * 2, v.tensor_reduce(var, h, AX.X, ALU.add), 1)
                    dve.wait_ge(n2_r, kb * 2 + 2)
                    own(n2, kb * 2, v.tensor_tensor(h, x1c[:].rearrange("p t w (s f) -> p (t w s) f", s=SETS),
                                                    r.unsqueeze(2).broadcast_to([P, 3 * CW * SETS, EMB]), ALU.mult), 2)

                def scores(p):
                    k = p.chunk
                    dve.wait_ge(q_read, k * TW + TW + 2)
                    for n, d in enumerate((-1, 0, 1)):
                        query_key(nc.vector, d).then_inc(sc_v, 1)
                    for n, d in enumerate((-1, 0, 1, -2, 2)):
                        if n < 3:
                            dve.wait_ge(sc_v, k * 8 + n + 1)
                        else:
                            dve.wait_ge(sc_p, k * 2 + n - 2)
                        lo, m = max(0, -d), TW - abs(d)
                        v.tensor_reduce(Sc[:, d + 2, lo:lo + m, :],
                                        scratch(d)[:, 0:m, :].rearrange("p w (g e) -> p w g e", e=HEAD),
                                        AX.X, ALU.add).then_inc(sc_v, 1)
                    dve.wait_ge(sc_v, k * 8 + 8)

                def softmax_shift(p):
                    k, b = p.chunk, p.chunk * 9
                    top = sm[:, 0, :].rearrange("p (d n) -> p d n", d=3)
                    for d in range(3):
                        s = Sc[:, 2 - d:5 - d, d:d + CW, :].rearrange("p e w g -> p e (w g)")
                        own(soft, b, v.tensor_reduce(top[:, d, :], s.rearrange("p e n -> p n e"), AX.X, ALU.max), 2 * d + 1)
                        own(soft, b, v.tensor_tensor(At[:, d, :, :], s, top[:, d, :].unsqueeze(1).broadcast_to([P, 3, CW * SH]),
                                                     ALU.subtract), 2 * d + 2)

                def softmax_scale(p):
                    k, b = p.chunk, p.chunk * 9
                    dve.wait_ge(soft_exp, k + 1)
                    own(soft, b, v.tensor_reduce(sm[:, 1, :].rearrange("p (d n) -> p d n", d=3),
                                                 At[:].rearrange("p d e n -> p d n e"), AX.X, ALU.add), 7)
                    own(soft, b, v.reciprocal(sm[:, 2, :], sm[:, 1, :]), 8)
                    own(soft, b, v.tensor_tensor(At[:], At[:], sm[:, 2, :].rearrange("p (d n) -> p d n", d=3).unsqueeze(2)
                                                 .broadcast_to([P, 3, 3, CW * SH]), ALU.mult), 9)

                def values(p, d):
                    k = p.chunk
                    for e in range(3):
                        out = PR[:, 3 * d + e, :].rearrange("p (w g n) -> p w g n", g=SH, n=HEAD)
                        a = At[:, d, e, :].rearrange("p (w g) -> p w g", g=SH).unsqueeze(3).broadcast_to([P, CW, SH, HEAD])
                        val = QKV[:, e:e + CW, 2 * F2:3 * F2].rearrange("p w (g n) -> p w g n", n=HEAD)
                        v.tensor_tensor(out, val, a, ALU.mult).then_inc(val_v, 1)

                def add_attention(p):
                    for g in range(6):
                        c = p.c["proj"] + g
                        d, w = g // 2, (g % 2) * 4
                        dve.wait_ge(c_made, p.c_base + c + 1)
                        v.tensor_tensor(x1c[:, d, w:w + 4, :], cps[:, c % 2, 0:4 * F2].rearrange("p (w f) -> p w f", f=F2),
                                        Tc[:, d + w:d + w + 4, :], ALU.add).then_inc(c_read, 1)

                def add_mlp(p, g):
                    c = p.c["mlp"] + g
                    d, w = g // 2, (g % 2) * 4
                    dve.wait_ge(c_made, p.c_base + c + 1)
                    v.tensor_tensor(x2c[:, d, w:w + 4, :], cps[:, c % 2, 0:4 * F2].rearrange("p (w f) -> p w f", f=F2),
                                    x1c[:, d, w:w + 4, :], ALU.add).then_inc(c_read, 1)

                def norm_out(p):
                    kb, b = p.behind, p.behind * 4
                    var, r = st[:, 6, :], st[:, 7, :]
                    h = x2c[:].rearrange("p t w (s f) -> p (t w s) f", s=SETS)
                    dve.wait_ge(n3_sq, kb + 1)
                    own(n3, b, v.tensor_reduce(var, hB[:].rearrange("p t w (s f) -> p (t w s) f", s=SETS), AX.X, ALU.add), 1)
                    dve.wait_ge(n3_r, kb * 2 + 2)
                    own(n3, b, v.tensor_tensor(h, h, r.unsqueeze(2).broadcast_to([P, 3 * CW * SETS, EMB]), ALU.mult), 2)
                    dve.wait_ge(t_read, p.t_base + 2)
                    own(n3, b, v.tensor_tensor(zs[:], x2c[:, 0], x2c[:, 1], ALU.add), 3)
                    own(n3, b, v.tensor_tensor(zs[:], zs[:], x2c[:, 2], ALU.add), 4)

                def add_conv(p, t):
                    w0 = (NCHUNK - 1) * CW if t is None else (t - 1) * CW
                    for g in range(2):
                        c = p.c["conv"] + g
                        dve.wait_ge(c_made, p.c_base + c + 1)
                        x = XB[:, :, bass.ds(w0 + g * 4, 4)]
                        v.tensor_tensor(x, cps[:, c % 2, 0:P].rearrange("p (w o) -> p o w", w=4), x, ALU.add).then_inc(c_read, 1)

                def body(p, t=None):
                    if p.attn:
                        if not p.mlp:
                            dve.wait_ge(tb_in, p.pair * (10 * 16) + 10 * 16)
                        norm_tokens(p, t)
                    if p.mlp:
                        norm_residual(p)
                    if p.attn:
                        scores(p)
                        softmax_shift(p)
                    if p.mlp:
                        add_mlp(p, 0)
                    if p.attn:
                        softmax_scale(p)
                    for d in range(3):
                        if p.attn:
                            values(p, d)
                        if p.mlp:
                            add_mlp(p, 1 + d)
                    if p.mlp:
                        add_mlp(p, 4)
                        add_mlp(p, 5)
                        norm_out(p)
                    if p.attn:
                        if not p.mlp:
                            dve.wait_ge(xb_in, p.pair * (SETS * 16) + SETS * 16)
                            v.tensor_tensor(XB[:], XB[:], cbias[:].unsqueeze(2).broadcast_to([P, SETS * C, W]), ALU.add).then_inc(xb_ready, 1)
                            dve.wait_ge(xb_ready, p.pair + 1)
                        add_attention(p)
                    if p.mlp:
                        add_conv(p, t)

                steps(dve, body)

            @block.gpsimd
            def _(pool):
                g_ = nc.gpsimd

                def body(p, t=None):
                    if not p.attn:
                        return
                    k = p.chunk
                    pool.wait_ge(q_read, k * TW + TW + 2)
                    pool.wait_ge(c_read, p.c_base + 2)
                    for d in (-2, 2):
                        query_key(g_, d).then_inc(sc_p, 1)
                    for d in range(3):
                        y = PR[:, 3 * d, :]
                        for e in (1, 2):
                            pool.wait_ge(val_v, k * 9 + 3 * d + e + 1)
                            if e == 2:
                                pool.wait_ge(val_p, k * 6 + 2 * d + 1)
                            g_.tensor_tensor(y, y, PR[:, 3 * d + e, :], ALU.add).then_inc(val_p, 1)

                steps(pool, body)

            @block.scalar
            def _(act):
                s_ = nc.scalar
                act.sem_inc(t_read, 2)
                act.sem_inc(q_read, 2)
                act.sem_inc(f_read, 2)
                act.wait_ge(w_ready, 2)

                def inverse_std(var, r, sem_, base):
                    s_.activation(r, var, ACT.Ln, bias=eps[:], scale=1.0 / EMB).then_inc(sem_, 1)
                    act.wait_ge(sem_, base + 1)
                    s_.activation(r, r, ACT.Exp, scale=-0.5).then_inc(sem_, 1)

                def read_t(p, name, g, out, n):
                    k = p.t[name] + g
                    act.wait_ge(t_made, p.t_base + k + 1)
                    s_.activation(out, tps[0:F2, k % 2, 0:n * P].rearrange("f (w h) -> f w h", h=P), ACT.Copy).then_inc(t_read, 1)

                def gelu(p, g):
                    kb = p.behind
                    act.wait_ge(c_made, p.c_base + (p.c["mlp"] + g - 1 if g >= 2 else 0))
                    for m in range(3):
                        n = g * 3 + m
                        act.wait_ge(f_made, kb * 18 + n + 1)
                        s_.activation(G[:, g % 2, m, :], fps[:, n % 2, :], ACT.Gelu).then_inc(f_read, 1)

                def body(p, t=None):
                    if p.mlp:
                        kb = p.behind
                        act.wait_ge(c_read, p.c_base + 2)
                        act.wait_ge(n3, kb * 4)
                        s_.activation(hB[:], x1c[:], ACT.Square).then_inc(n2_sq, 1)
                    if p.attn:
                        k = p.chunk
                        act.wait_ge(n1, k * 5 + 3)
                        s_.activation(hA[:], Tc[:], ACT.Square).then_inc(n1_sq, 1)
                        act.wait_ge(n1, k * 5 + 4)
                        inverse_std(st[:, 2, 0:TW * SETS], st[:, 3, 0:TW * SETS], n1_r, k * 2)
                    if p.mlp:
                        act.wait_ge(n2, kb * 2 + 1)
                        inverse_std(st[:, 4, :], st[:, 5, :], n2_r, kb * 2)
                    if p.attn:
                        at = 0
                        for g, n in enumerate(T_WIDTHS):
                            read_t(p, "norm1", g, hAT[:, at:at + n, :], n)
                            at += n
                        act.wait_ge(val_v, k * 9)
                        for w in range(TW):
                            act.wait_ge(q_made, k * TW + w + 1)
                            s_.activation(QKV[:, w, :], qps[:, w % 2, 0:3 * F2], ACT.Copy).then_inc(q_read, 1)
                    if p.mlp:
                        for g in range(6):
                            read_t(p, "norm2", g, hBT[:, g * 4:(g + 1) * 4, :], 4)
                        gelu(p, 0)
                        gelu(p, 1)
                    if p.attn:
                        act.wait_ge(soft, k * 9 + 6)
                        s_.activation(At[:], At[:], ACT.Exp, scale=float(HEAD) ** -0.5).then_inc(soft_exp, 1)
                    if p.mlp:
                        for g in range(2, 6):
                            gelu(p, g)
                        act.wait_ge(c_read, p.c_base + p.c["mlp"] + 6 + 2)
                        s_.activation(hB[:], x2c[:], ACT.Square).then_inc(n3_sq, 1)
                    if p.attn:
                        act.wait_ge(c_read, p.c_base + 2)
                        for g in range(6):
                            read_t(p, "mix", g, yT[:, g // 2, (g % 2) * 4:(g % 2) * 4 + 4, :], 4)
                    if p.mlp:
                        act.wait_ge(n3, kb * 4 + 1)
                        inverse_std(st[:, 6, :], st[:, 7, :], n3_r, kb * 2)
                        for g in range(2):
                            read_t(p, "norm3", g, zT[:, g * 4:(g + 1) * 4, :], 4)

                steps(act, body)


def layer1(nc, x1, x2, pw, pair, w1):
    TILE = 1024
    NT = HW // TILE
    LOADS = 8
    with ExitStack() as ctx:
        def sb(name, shape, dt=F32):
            return ctx.enter_context(nc.sbuf_tensor(name, shape, dt))

        def sem(name):
            return ctx.enter_context(nc.semaphore(name))

        X = sb("l1_x", [P, HW])
        with ExitStack() as ctx1:
            def sb1(name, shape, dt=F32):
                return ctx1.enter_context(nc.sbuf_tensor(name, shape, dt))

            norm = Norm(nc, ctx1, "n1")
            G = sb1("l1_g", [P, HW])
            mats = sb1("l1_mats", [P, 5, P])
            vecs = sb1("l1_vecs", [P, 5])
            top = sb1("l1_top", [P, 8])
            stat = sb1("l1_stat", [P, 8])
            scaled = sb1("l1_scaled", [P, 2, P])
            fold = sb1("l1_fold", [P, 2, P])
            bias = sb1("l1_bias", [P, 2])
            gate = sb1("l1_gate", [P, 2, 2, TILE])
            mix = sb1("l1_mix", [P, 2, TILE])
            fps = ctx1.enter_context(nc.psum_tensor("l1_fps", [P, 2, 132], F32))
            gps = ctx1.enter_context(nc.psum_tensor("l1_gps", [P, 2, 2, 512], F32))
            ops = ctx1.enter_context(nc.psum_tensor("l1_ops", [P, 2, 512], F32))
            x_in = [sem(f"l1_x_in{k}") for k in range(LOADS)]
            w_in = sem("l1_w_in")
            chain = sem("l1_chain")
            top_chain = sem("l1_top_chain")
            g_ready = sem("l1_g_ready")
            scaled_ready = sem("l1_scaled_ready")
            fold_made = sem("l1_fold_made")
            fold_ready = sem("l1_fold_ready")
            pre_made = sem("l1_pre_made")
            tanh_done = sem("l1_tanh_done")
            gates_ready = sem("l1_gates_ready")
            sum_done = sem("l1_sum_done")
            mix_ready = sem("l1_mix_ready")
            out_made = sem("l1_out_made")
            out_done = sem("l1_out_done")
            stored = sem("l1_stored")
            with nc.Block() as block:
                @block.sync
                def _(sp):
                    for k in range(LOADS):
                        n = HW // LOADS
                        sp.dma_start(X[:, k * n:(k + 1) * n], x1[:, k * n:(k + 1) * n]).then_inc(x_in[k], 16)
                    norm.sync_part(sp, pair)
                    sp.dma_start(mats[:], w1[0]).then_inc(w_in, 16)
                    sp.dma_start(vecs[:], w1[1]).then_inc(w_in, 16)
                    for k in range(4):
                        n = HW // 4
                        sp.wait_ge(out_done, (k + 1) * NT // 4)
                        sp.dma_start(x2[:, k * n:(k + 1) * n], X[:, k * n:(k + 1) * n]).then_inc(stored, 16)
                    sp.wait_ge(stored, 4 * 16)

                @block.vector
                def _(dve):
                    v = nc.vector
                    link = Chain(dve, chain)

                    def chunk_in(e, k):
                        if k % (norm.CHUNKS // LOADS) == 0:
                            e.wait_ge(x_in[k // (norm.CHUNKS // LOADS)], 16)

                    norm.vector_part(dve, link, lambda k, n: X[:, k * n:(k + 1) * n], chunk_in)
                    link(v.reduce_max(top[:, 0:1], X[:], AX.X))
                    link(v.tensor_scalar(stat[:, 0:1], norm.own[:, 0:1], norm.rstd[:], norm.shift[:], ALU.mult, ALU.add))
                    link(v.tensor_scalar(stat[:, 1:2], top[:, 0:1], norm.rstd[:], norm.shift[:], ALU.mult, ALU.add))
                    link(v.tensor_scalar(stat[:, 2:4], stat[:, 0:2], 1e-5, None, ALU.add))
                    link(v.reciprocal(stat[:, 4:6], stat[:, 2:4]))
                    dve.wait_ge(w_in, 32)
                    for m in range(2):
                        last = v.tensor_scalar(scaled[:, m, :], mats[:, 2 + m, :], stat[:, 4 + m:5 + m], None, ALU.mult)
                    last.then_inc(scaled_ready, 1)
                    dve.wait_ge(fold_made, 1)
                    v.tensor_copy(fold[:], fps[:, :, 0:P])
                    link(v.tensor_tensor(bias[:], fps[:, :, P], vecs[:, 2:4], ALU.add))
                    v.tensor_scalar(G[:], X[:], norm.rstd[:], norm.shift[:], ALU.mult, ALU.add).then_inc(g_ready, 1)
                    with dve.Fori(0, NT // 2) as it:
                        for j in range(2):
                            at = it * (2 * TILE) + j * TILE
                            dve.wait_ge(gates_ready, it * 2 + j + 1)
                            v.scalar_tensor_tensor(gate[:, j, 0, :], gate[:, j, 0, :], 1.0, gate[:, j, 1, :],
                                                   ALU.add, ALU.add).then_inc(sum_done, 1)
                            dve.wait_ge(sum_done, it * 2 + j + 1)
                            v.tensor_tensor(mix[:, j, :], gate[:, j, 0, :], G[:, bass.ds(at, TILE)],
                                            ALU.mult).then_inc(mix_ready, 1)
                            dve.wait_ge(out_made, it * 2 + j + 1)
                            xt = X[:, bass.ds(at, TILE)]
                            v.scalar_tensor_tensor(xt, ops[:].rearrange("p a n -> p (a n)"), vecs[:, 4:5], xt,
                                                   ALU.add, ALU.add).then_inc(out_done, 1)

                @block.tensor
                def _(pe):
                    t = nc.tensor
                    norm.tensor_part(pe)
                    pe.wait_ge(scaled_ready, 1)
                    for m in range(2):
                        t.matmul(fps[:, m, 0:P], mats[:, m, :], scaled[:, m, :], start=True, stop=True)
                        last = t.matmul(fps[:, m, P:P + 1], scaled[:, m, :], vecs[:, m:m + 1], start=True, stop=True)
                    last.then_inc(fold_made, 1)
                    pe.wait_ge(g_ready, 1)
                    with pe.Fori(0, NT // 2) as it:
                        for j in range(2):
                            at = it * (2 * TILE) + j * TILE
                            for m in range(2):
                                pe.wait_ge(tanh_done, it * 4 + j * 2 + m)
                                for q in range(2):
                                    last = t.matmul(gps[:, m, q, :], fold[:, m, :], G[:, bass.ds(at + q * 512, 512)],
                                                    start=True, stop=True)
                                last.then_inc(pre_made, 1)
                            pe.wait_ge(mix_ready, it * 2 + j + 1)
                            for q in range(2):
                                last = t.matmul(ops[:, q, :], mats[:, 4, :], mix[:, j, q * 512:(q + 1) * 512],
                                                start=True, stop=True)
                            last.then_inc(out_made, 1)

                @block.scalar
                def _(act):
                    s = nc.scalar
                    norm.scalar_part(act)
                    act.wait_ge(g_ready, 1)
                    with act.Fori(0, NT // 2) as it:
                        for j in range(2):
                            act.wait_ge(mix_ready, it * 2 + j - 1) if j else act.wait_ge(mix_ready, it * 2)
                            for m in range(2):
                                act.wait_ge(pre_made, it * 4 + j * 2 + m + 1)
                                s.activation(gate[:, j, m, :], gps[:, m, :, :].rearrange("p a n -> p (a n)"),
                                             ACT.Tanh, bias=bias[:, m:m + 1]).then_inc(tanh_done, 1)
                            act.wait_ge(tanh_done, it * 4 + j * 2 + 2)
                            s.activation(gate[:, j, :, :], gate[:, j, :, :], ACT.Sigmoid).then_inc(gates_ready, 1)

        powers(nc, ctx, X, pw, pair)


def powers(nc, ctx, X, pw, pair):
    CH = SUB
    NCH = IMG // CH
    BUF = 3
    STORES = 3 * DEG
    with ExitStack() as ctx2:
        def sb(name, shape, dt=F32):
            return ctx2.enter_context(nc.sbuf_tensor(name, shape, dt))

        def sem(name):
            return ctx2.enter_context(nc.semaphore(name))

        norm = Norm(nc, ctx2, "n2")
        GP = sb("pw_g", [P, IMG])
        up = sb("pw_up", [P, DEG - 1, CH])
        hi = sb("pw_hi", [P, BUF, DEG, CH], BF16)
        mid = sb("pw_mid", [P, BUF, DEG, CH], BF16)
        lo = sb("pw_lo", [P, BUF, DEG, CH], BF16)
        rest = sb("pw_rest", [P, DEG, CH])
        chain = sem("pw_chain")
        zeroed = sem("pw_zeroed")
        padded = sem("pw_padded")
        up_ready = sem("pw_up_ready")
        hi_ready = sem("pw_hi_ready")
        rest_ready = sem("pw_rest_ready")
        mid_ready = sem("pw_mid_ready")
        lo_ready = sem("pw_lo_ready")
        stored = [sem(f"pw_stored{u}") for u in range(BUF)]
        with nc.Block() as block:
            @block.sync
            def _(sp):
                norm.sync_part(sp, pair)
                lines = pw.rearrange("t c i (b n) -> t i b c n", b=NB)
                with sp.Fori(0, NCH // BUF) as it:
                    for u in range(BUF):
                        k = it * BUF + u
                        for part, (t, ready) in enumerate(((hi, hi_ready), (mid, mid_ready), (lo, lo_ready))):
                            sp.wait_ge(ready, k * DEG + DEG)
                            for i in range(DEG):
                                sp.dma_start(lines[part, i, :, :, bass.ds(k * CH, CH)], t[:, u, i, :]).then_inc(stored[u], 16)
                for u in range(BUF):
                    sp.wait_ge(stored[u], NCH // BUF * STORES * 16)

            @block.gpsimd
            def _(pool):
                nc.gpsimd.memset(GP[:], 0.0).then_inc(zeroed, 1)

            @block.vector
            def _(dve):
                v = nc.vector
                link = Chain(dve, chain)
                norm.vector_part(dve, link, lambda k, n: X[:, k * n:(k + 1) * n], lambda e, k: None)
                dve.wait_ge(zeroed, 1)
                v.tensor_scalar(image_rows(GP), X[:].rearrange("p (h w) -> p h w", w=W), norm.rstd[:], norm.shift[:],
                                ALU.mult, ALU.add).then_inc(padded, 1)
                dve.wait_ge(padded, 1)
                with dve.Fori(0, NCH // BUF) as it:
                  for u in range(BUF):
                    k = it * BUF + u
                    g = GP[:, bass.ds(k * CH, CH)]
                    of = [g] + [up[:, i, :] for i in range(DEG - 1)]
                    for i, (a, b) in enumerate(((0, 0), (1, 0), (1, 1), (3, 0))):
                        v.tensor_tensor(up[:, i, :], of[a], of[b], ALU.mult).then_inc(up_ready, 1)
                        dve.wait_ge(up_ready, k * (DEG - 1) + i + 1)
                    for i in range(DEG):
                        dve.wait_ge(hi_ready, k * DEG + i + 1)
                        v.tensor_tensor(rest[:, i, :], of[i], hi[:, u, i, :], ALU.subtract).then_inc(rest_ready, 1)
                    dve.wait_ge(stored[u], it * (STORES * 16))
                    for i in range(DEG):
                        dve.wait_ge(mid_ready, k * DEG + i + 1)
                        v.tensor_tensor(lo[:, u, i, :], rest[:, i, :], mid[:, u, i, :], ALU.subtract).then_inc(lo_ready, 1)
                    dve.wait_ge(lo_ready, k * DEG + DEG)

            @block.tensor
            def _(pe):
                norm.tensor_part(pe)

            @block.scalar
            def _(act):
                s = nc.scalar
                norm.scalar_part(act)
                act.wait_ge(padded, 1)
                with act.Fori(0, NCH // BUF) as it:
                  for u in range(BUF):
                    k = it * BUF + u
                    act.wait_ge(stored[u], it * (STORES * 16))
                    for i in range(DEG):
                        if i:
                            act.wait_ge(up_ready, k * (DEG - 1) + i)
                        src = up[:, i - 1, :] if i else GP[:, bass.ds(k * CH, CH)]
                        s.activation(hi[:, u, i, :], src, ACT.Copy).then_inc(hi_ready, 1)
                    for i in range(DEG):
                        act.wait_ge(rest_ready, k * DEG + i + 1)
                        s.activation(mid[:, u, i, :], rest[:, i, :], ACT.Copy).then_inc(mid_ready, 1)


NPP = len(AROUND) // 2
NPAIRED = NCG * NPP
NBLK = NPAIRED + 2
BODY = 6
SUBS = BODY * NSUB
STEPS = SUBS * NBLK
Q_BANKS, P_BANKS, A_RING, R_RING = 2, 3, 6, 9
assert NBLK % Q_BANKS == 0 and NBLK % P_BANKS == 0 and NBLK % A_RING == 0 and NBLK % R_RING == 0
ABS_DVE = {1, 5, 9, 13, 16}
SQ_DVE = {3, 8, 15}
SQ_ACT = {6, 12}
LAG_P, LAG_SUM, LAG_MUL = 3, 6, 4
LOADED = SLOTS * NSUB * NBLK


def among(members, s):
    return (s // NBLK) * len(members) + sum(n <= s % NBLK for n in members)


def layer2(nc, pw, l2w, out2):
    all_blocks = set(range(NBLK))
    abs_act = all_blocks - ABS_DVE
    sq_pool = all_blocks - SQ_DVE - SQ_ACT
    wcols = NPAIRED * P + NCG * P
    with ExitStack() as ctx:
        def sb(name, shape, dt=F32):
            return ctx.enter_context(nc.sbuf_tensor(name, shape, dt))

        def sem(name):
            return ctx.enter_context(nc.semaphore(name))

        wst = sb("l2_wst", [KROWS, 2, wcols], BF16)
        with ExitStack() as ctx0:
            raw = ctx0.enter_context(nc.sbuf_tensor("l2_raw", [KROWS, 2, wcols], F32))
            part = ctx0.enter_context(nc.sbuf_tensor("l2_part", [KROWS, wcols], BF16))
            total = ctx0.enter_context(nc.sbuf_tensor("l2_total", [KROWS, wcols], F32))
            mask = ctx0.enter_context(nc.sbuf_tensor("l2_mask", [KROWS, 3], F32))
            w_in = sem("l2_w_in")
            wchain = sem("l2_wchain")
            with nc.Block() as block:
                @block.sync
                def _(sp):
                    for k in range(2):
                        sp.dma_start(raw[:, k, :], l2w[k]).then_inc(w_in, 16)
                    sp.dma_start(mask[:], l2w[2]).then_inc(w_in, 16)

                @block.vector
                def _(dve):
                    v = nc.vector
                    link = Chain(dve, wchain)
                    dve.wait_ge(w_in, 48)
                    for k in range(2):
                        link(v.tensor_copy(part[:], raw[:, k, :]))
                        link(v.tensor_scalar(total[:], part[:], mask[:, 0:1], None, ALU.mult))
                        for m in (1, 2):
                            link(v.tensor_tensor(raw[:, k, :], raw[:, k, :], part[:], ALU.subtract))
                            link(v.tensor_copy(part[:], raw[:, k, :]))
                            link(v.scalar_tensor_tensor(total[:], part[:], mask[:, m:m + 1], total[:], ALU.mult, ALU.add))
                        link(v.tensor_copy(wst[:, k, :], total[:]))

        sums = sb("l2_sums", [P, 2, 32])
        pick = sb("l2_pick", [P, len(AROUND), 32])
        mv = sb("l2_mv", [KROWS, SLOTS, NCG, SUP], BF16)
        A = sb("l2_a", [P, A_RING, SUB])
        R = sb("l2_r", [P, R_RING, SUB])
        S = sb("l2_s", [P, SLOTS, SUP])
        O = sb("l2_o", [P, 2, SUB])
        qps = ctx.enter_context(nc.psum_tensor("l2_qps", [P, Q_BANKS, 512], F32))
        pps = ctx.enter_context(nc.psum_tensor("l2_pps", [P, P_BANKS, 512], F32))
        sps = ctx.enter_context(nc.psum_tensor("l2_sps", [P, 512], F32))
        ops = ctx.enter_context(nc.psum_tensor("l2_ops", [P, 2, 512], F32))
        c_in = sem("l2_c_in")
        mv_in = [sem(f"l2_mv_in{k}") for k in range(SLOTS)]
        cleared = sem("l2_cleared")
        q_made = sem("l2_q_made")
        p_made = sem("l2_p_made")
        abs_a, abs_v = sem("l2_abs_a"), sem("l2_abs_v")
        root_done = sem("l2_root_done")
        sq_a, sq_v, sq_p = sem("l2_sq_a"), sem("l2_sq_v"), sem("l2_sq_p")
        mul_done = sem("l2_mul_done")
        summed = sem("l2_summed")
        s_copied = sem("l2_s_copied")
        o_made, o_copied = sem("l2_o_made"), sem("l2_o_copied")
        stored = [sem("l2_stored0"), sem("l2_stored1")]

        def wait_abs(e, it, s):
            if s % NBLK in ABS_DVE:
                e.wait_ge(abs_v, it * (SUBS * len(ABS_DVE)) + among(ABS_DVE, s))
            else:
                e.wait_ge(abs_a, it * (SUBS * len(abs_act)) + among(abs_act, s))

        def wait_square(e, it, s):
            for members, done in ((SQ_DVE, sq_v), (SQ_ACT, sq_a), (sq_pool, sq_p)):
                if s % NBLK in members:
                    e.wait_ge(done, it * (SUBS * len(members)) + among(members, s))

        with nc.Block() as block:
            @block.sync
            def _(sp):
                sp.dma_start(sums[:], l2w[3]).then_inc(c_in, 16)
                sp.dma_start(pick[:], l2w[4]).then_inc(c_in, 16)
                sp.wait_ge(cleared, 3)
                with sp.Fori(0, NSUP // BODY) as it:
                    for u in range(BODY):
                        sp.wait_ge(p_made, (it * BODY + u + 1) * (NBLK * NSUB))
                        at = (it * BODY + u) * SUP
                        rows = 0
                        for x_part, times in ((0, 3), (1, 2), (2, 1)):
                            for r in range(times):
                                for cg in range(NCG):
                                    src = pw[x_part, cg * CG:(cg + 1) * CG, :, bass.ds(at, SUP)].rearrange("c i n -> (c i) n")
                                    sp.dma_start(mv[rows:rows + CG * DEG, u % SLOTS, cg, :], src).then_inc(mv_in[u % SLOTS], 16)
                                rows += CG * DEG

            @block.gpsimd
            def _(pool):
                g = nc.gpsimd
                g.memset(mv[:], 1.0).then_inc(cleared, 1)
                g.memset(S[:], 0.0).then_inc(cleared, 1)
                g.memset(O[:], 0.0).then_inc(cleared, 1)
                pool.wait_ge(cleared, 3)
                with pool.Fori(0, NSUP // BODY) as it:
                    for s in range(STEPS):
                        if s % NBLK in sq_pool:
                            a = A[:, s % A_RING, :]
                            pool.wait_ge(root_done, it * STEPS + s + 1)
                            g.tensor_tensor(a, a, a, ALU.mult).then_inc(sq_p, 1)

            @block.tensor
            def _(pe):
                t = nc.tensor

                def product(k, s, out):
                    sub, n = divmod(s, NBLK)
                    cols = slice((sub % NSUB) * SUB, (sub % NSUB + 1) * SUB)
                    x = mv[:, (sub // NSUB) % SLOTS]
                    if n < NPAIRED:
                        return t.matmul(out, wst[:, k, n * P:(n + 1) * P], x[:, n // NPP, cols], start=True, stop=True)
                    for cg in (2 * (n - NPAIRED), 2 * (n - NPAIRED) + 1):
                        at = NPAIRED * P + cg * P
                        last = t.matmul(out, wst[:, k, at:at + P], x[:, cg, cols],
                                        start=cg % 2 == 0, stop=cg % 2 == 1)
                    return last

                def shifted_sums(bank, slot):
                    for k, p in enumerate(AROUND):
                        for j in range(NSUB):
                            a = 0
                            while a < SUB:
                                src = j * SUB + OFFS[p] + a
                                where, src = src // SUP, src % SUP
                                n = min(SUB - a, SUP - src)
                                last = t.matmul(ops[32 * j:32 * j + 32, bank, a:a + n], pick[:, k, :],
                                                S[:, (slot + where) % SLOTS, src:src + n],
                                                start=False, stop=k == len(AROUND) - 1, skip_group_check=True)
                                a += n
                    last.then_inc(o_made, 1)

                pe.sem_inc(p_made, LOADED)
                pe.sem_inc(summed, R_RING)
                pe.wait_ge(c_in, 32)
                pe.wait_ge(cleared, 3)
                for j in range(NSUB):
                    t.matmul(ops[32 * j:32 * j + 32, 1, 0:SUB], sums[:, 0, :], S[:, 2, 0:SUB], start=True, stop=False,
                             skip_group_check=True)
                with pe.Fori(0, NSUP // BODY) as it:
                    for s in range(STEPS + LAG_SUM):
                        sub, n = divmod(s, NBLK)
                        if s < STEPS:
                            if n == 0 and sub % NSUB == 0:
                                u = sub // NSUB
                                pe.wait_ge(mv_in[u % SLOTS], (it * (BODY // SLOTS) + u // SLOTS + 1) * (6 * NCG * 16))
                            if s >= Q_BANKS:
                                wait_abs(pe, it, s - Q_BANKS)
                            product(1, s, qps[:, s % Q_BANKS, 0:SUB]).then_inc(q_made, 1)
                        m = s - LAG_P
                        if 0 <= m < STEPS:
                            pe.wait_ge(mul_done, it * STEPS + m - P_BANKS + 1 + A_RING)
                            product(0, m, pps[:, m % P_BANKS, 0:SUB]).then_inc(p_made, 1)
                        m = s - LAG_SUM
                        if m < 0:
                            continue
                        sub, n = divmod(m, NBLK)
                        u, j = divmod(sub, NSUB)
                        if n < NPAIRED and n % NPP == NPP - 1:
                            pe.wait_ge(mul_done, it * STEPS + m + 1 + A_RING)
                            if n == NPP - 1:
                                pe.wait_ge(s_copied, it * SUBS + sub)
                            for pp in range(NPP):
                                last = t.matmul(sps[32 * pp:32 * pp + 32, 0:SUB], sums[:, 0, :],
                                                R[:, (m - NPP + 1 + pp) % R_RING, :], start=n == NPP - 1,
                                                stop=n == NPAIRED - 1, skip_group_check=True)
                            last.then_inc(summed, NPP)
                        if n >= NPAIRED:
                            pe.wait_ge(mul_done, it * STEPS + m + 1 + A_RING)
                            if n == NPAIRED and j == 0:
                                pe.wait_ge(o_copied, it * BODY + u)
                            t.matmul(ops[32 * j:32 * j + 32, u % 2, 0:SUB], sums[:, 1, :], R[:, m % R_RING, :],
                                     start=n == NPAIRED, stop=False, skip_group_check=True).then_inc(summed, 1)
                        if m % (NBLK * NSUB) == 2 * NBLK - 4:
                            pe.wait_ge(s_copied, it * SUBS + u * NSUB + 1)
                            shifted_sums((u + 1) % 2, (u - 1) % SLOTS)
                pe.wait_ge(s_copied, NSUP * NSUB)
                shifted_sums(1, (BODY - 1) % SLOTS)

            @block.vector
            def _(dve):
                v = nc.vector
                dve.sem_inc(mul_done, A_RING)
                with dve.Fori(0, NSUP // BODY) as it:
                    for s in range(STEPS + LAG_MUL):
                        if s < STEPS and s % NBLK in ABS_DVE:
                            dve.wait_ge(q_made, it * STEPS + s + 1)
                            dve.wait_ge(mul_done, it * STEPS + s + 1)
                            v.tensor_scalar(A[:, s % A_RING, :].bitcast(I32), qps[:, s % Q_BANKS, 0:SUB].bitcast(I32),
                                            0x7FFFFFFF, None, ALU.bitwise_and).then_inc(abs_v, 1)
                        m = s - 3
                        if 0 <= m < STEPS and m % NBLK in SQ_DVE:
                            a = A[:, m % A_RING, :]
                            dve.wait_ge(root_done, it * STEPS + m + 1)
                            v.tensor_tensor(a, a, a, ALU.mult).then_inc(sq_v, 1)
                        m = s - LAG_MUL
                        if 0 <= m < STEPS:
                            wait_square(dve, it, m)
                            dve.wait_ge(p_made, it * STEPS + m + 1 + LOADED)
                            dve.wait_ge(summed, it * STEPS + m + 1)
                            v.tensor_tensor(R[:, m % R_RING, :], pps[:, m % P_BANKS, 0:SUB], A[:, m % A_RING, :],
                                            ALU.mult).then_inc(mul_done, 1)

            @block.scalar
            def _(act):
                s_ = nc.scalar

                def copy_out(bank, n, done):
                    act.wait_ge(o_made, n + 1)
                    act.wait_ge(stored[bank], done)
                    s_.activation(O[:, bank, :], ops[:, bank, 0:SUB], ACT.Copy).then_inc(o_copied, 1)
                    act.wait_ge(o_copied, n + 1)

                def store(bank, n):
                    for j in range(NSUB):
                        act.dma_start(out2[:, bass.ds(n * SUP + j * SUB, SUB)], O[32 * j:32 * j + C, bank, :]).then_inc(stored[bank], 16)

                act.wait_ge(cleared, 3)
                with act.Fori(0, NSUP // BODY) as it:
                    for s in range(STEPS + 9):
                        if s < STEPS and s % NBLK in abs_act:
                            act.wait_ge(q_made, it * STEPS + s + 1)
                            act.wait_ge(mul_done, it * STEPS + s + 1)
                            s_.activation(A[:, s % A_RING, :], qps[:, s % Q_BANKS, 0:SUB], ACT.Abs).then_inc(abs_a, 1)
                        m = s - 1
                        if 0 <= m < STEPS:
                            a = A[:, m % A_RING, :]
                            wait_abs(act, it, m)
                            s_.activation(a, a, ACT.Abs_reciprocal_sqrt, bias=1.0).then_inc(root_done, 1)
                        m = s - 3
                        if 0 <= m < STEPS and m % NBLK in SQ_ACT:
                            a = A[:, m % A_RING, :]
                            act.wait_ge(root_done, it * STEPS + m + 1)
                            s_.activation(a, a, ACT.Square).then_inc(sq_a, 1)
                        m = s - 8
                        sub, n = divmod(m, NBLK)
                        if 0 <= m < STEPS and n == NPAIRED - 1:
                            act.wait_ge(summed, it * STEPS + m + 1 + R_RING)
                            u, j = divmod(sub, NSUB)
                            s_.activation(S[:, u % SLOTS, j * SUB:(j + 1) * SUB], sps[:, 0:SUB], ACT.Copy).then_inc(s_copied, 1)
                        if 0 <= m < STEPS and m % (NBLK * NSUB) == 2 * NBLK - 1:
                            u = m // (NBLK * NSUB)
                            copy_out((u + 1) % 2, it * BODY + u, (it * (BODY // 2) + u // 2) * (NSUB * 16))
                            store((u + 1) % 2, it * BODY + u)
                copy_out(1, NSUP, NSUP // 2 * NSUB * 16)
                store(1, NSUP)
                act.wait_ge(stored[0], NSUP // 2 * NSUB * 16)
                act.wait_ge(stored[1], (NSUP // 2 + 1) * NSUB * 16)


SPLINE = 8
GRID_STEP = 2.0 / 5


def layer3(nc, x2, out2, pair, l3w, x3q, g3q, s3q, oq, out):
    with ExitStack() as ctx:
        def sem(name):
            return ctx.enter_context(nc.semaphore(name))

        with ExitStack() as ctx1:
            def sb1(name, shape, dt=F32):
                return ctx1.enter_context(nc.sbuf_tensor(name, shape, dt))

            norm = Norm(nc, ctx1, "n3")
            X = sb1("l3_x", [P, HW])
            Y = sb1("l3_y", [P, IMG])
            XP = sb1("l3_xp", [P, IMG])
            zero = sb1("l3_zero", [C, MARGIN + SUP])
            x_in, y_in = sem("l3_x_in"), sem("l3_y_in")
            chain = sem("l3_chain")
            x_ready, g_ready, s_ready, zeroed = sem("l3_x_ready"), sem("l3_g_ready"), sem("l3_s_ready"), sem("l3_zeroed")
            x_stored, stored = sem("l3_x_stored"), sem("l3_stored")

            with nc.Block() as block:
                @block.sync
                def _(sp):
                    norm.sync_part(sp, pair)
                    sp.dma_start(X[:], x2).then_inc(x_in, 16)
                    for b in range(NB):
                        sp.dma_start(Y[b * C:(b + 1) * C, :], out2[:, SUP + b * IMG:SUP + (b + 1) * IMG]).then_inc(y_in, 16)
                    sp.wait_ge(x_ready, 1)
                    for b in range(NB):
                        sp.dma_start(x3q[:, SUP + b * IMG:SUP + (b + 1) * IMG], XP[b * C:(b + 1) * C, :]).then_inc(x_stored, 16)
                    sp.wait_ge(g_ready, 1)
                    for b in range(NB):
                        sp.dma_start(g3q[:, b * IMG:(b + 1) * IMG], Y[b * C:(b + 1) * C, :]).then_inc(stored, 16)
                    sp.wait_ge(s_ready, 1)
                    for b in range(NB):
                        sp.dma_start(s3q[:, MARGIN + SUP + b * IMG:MARGIN + SUP + (b + 1) * IMG], XP[b * C:(b + 1) * C, :]).then_inc(stored, 16)
                    sp.wait_ge(zeroed, 1)
                    sp.dma_start(x3q[:, 0:SUP], zero[:, 0:SUP]).then_inc(stored, 16)
                    sp.dma_start(s3q[:, 0:MARGIN + SUP], zero[:]).then_inc(stored, 16)
                    sp.dma_start(s3q[:, MARGIN + SUP + LINE:], zero[:, 0:MARGIN]).then_inc(stored, 16)
                    sp.wait_ge(x_stored, NB * 16)
                    sp.wait_ge(stored, (2 * NB + 3) * 16)

                @block.gpsimd
                def _(pool):
                    nc.gpsimd.memset(zero[:], 0.0).then_inc(zeroed, 1)

                @block.vector
                def _(dve):
                    v = nc.vector
                    link = Chain(dve, chain)
                    link(v.memset(XP[:], 0.0))
                    dve.wait_ge(x_in, 16)
                    dve.wait_ge(y_in, NB * 16)
                    link(v.tensor_tensor(X[:], X[:], image_rows(Y), ALU.add))
                    v.tensor_copy(image_rows(XP), X[:].rearrange("p (h w) -> p h w", w=W)).then_inc(x_ready, 1)
                    norm.vector_part(dve, link, lambda k, n: X[:, k * n:(k + 1) * n], lambda e, k: None)
                    link(v.memset(Y[:], 0.0))
                    v.tensor_scalar(image_rows(Y), X[:].rearrange("p (h w) -> p h w", w=W), norm.rstd[:], norm.shift[:],
                                    ALU.mult, ALU.add).then_inc(g_ready, 1)

                @block.tensor
                def _(pe):
                    norm.tensor_part(pe)

                @block.scalar
                def _(act):
                    norm.scalar_part(act)
                    act.wait_ge(g_ready, 1)
                    act.wait_ge(x_stored, NB * 16)
                    nc.scalar.activation(XP[:], Y[:], ACT.Silu).then_inc(s_ready, 1)

        def sb(name, shape, dt=F32):
            return ctx.enter_context(nc.sbuf_tensor(name, shape, dt))

        sw = sb("l3_sw", [P, 9, 9, C])
        scaler = sb("l3_scaler", [P, 9, 9, C])
        bw = sb("l3_bw", [P, 2, 9, C])
        wsp = sb("l3_wsp", [P, 9, 32])
        wba = sb("l3_wba", [P, 2, 32])
        place = sb("l3_place", [P, 1])
        ends = sb("l3_ends", [P, 2])
        cbias = sb("l3_cbias", [P, 1])
        gx = sb("l3_gx", [P, 2, SUP])
        a = sb("l3_a", [P, SUP])
        b = sb("l3_b", [P, SUP])
        a2 = sb("l3_a2", [P, SUP])
        b2 = sb("l3_b2", [P, SUP])
        B = sb("l3_bases", [P, BODY, SUP])
        si = sb("l3_si", [P, 2, SUP])
        si0 = sb("l3_si0", [P, 2, SUP])
        xr = sb("l3_xr", [P, 2, SUB])
        O = sb("l3_o", [P, 2, SUB])
        ops = ctx.enter_context(nc.psum_tensor("l3_ops", [P, 2, 512], F32))
        w_in = sem("l3_w_in")
        wchain = sem("l3_wchain")
        w_ready, cleared = sem("l3_w_ready"), sem("l3_cleared")
        gx_in = [sem("l3_gx_in0"), sem("l3_gx_in1")]
        si_in = [sem("l3_si_in0"), sem("l3_si_in1")]
        v_done, a_done, a2_done, b2_done = (sem(f"l3_{n}_done") for n in ("v", "a", "a2", "b2"))
        b_done = sem("l3_b_done")
        cube_a, cube_b, bases = sem("l3_cube_a"), sem("l3_cube_b"), sem("l3_bases_ready")
        o_made = sem("l3_o_made")
        o_done = sem("l3_o_done")
        out_stored = sem("l3_out_stored")
        stored = [sem("l3_o_stored0"), sem("l3_o_stored1")]
        STORE = NSUB * 16
        with nc.Block() as block:
            @block.sync
            def _(sp):
                for t, src in ((sw, l3w[0]), (scaler, l3w[1]), (bw, l3w[2]), (place, l3w[3]), (cbias, l3w[4])):
                    sp.dma_start(t[:], src).then_inc(w_in, 16)
                sp.wait_ge(cleared, 7)

                def load_bases_input(g, k, used):
                    sp.wait_ge(b_done, used)
                    for r in range(SPLINE):
                        sp.dma_start(gx[r * C:(r + 1) * C, k, :], g3q[:, bass.ds(g * SUP, SUP)]).then_inc(gx_in[k], 16)

                def load_silu(g, k):
                    sp.wait_ge(o_done, g + 1)
                    for r, p in enumerate(AROUND):
                        sp.dma_start(si[r * C:(r + 1) * C, k, :], s3q[:, bass.ds(g * SUP + (MARGIN + OFFS[p]), SUP)]).then_inc(si_in[k], 16)
                    sp.dma_start(si0[0:C, k, :], s3q[:, bass.ds(g * SUP + MARGIN, SUP)]).then_inc(si_in[k], 16)
                    for j in range(NSUB):
                        sp.dma_start(xr[32 * j:32 * j + C, k, :], x3q[:, bass.ds(g * SUP + j * SUB, SUB)]).then_inc(si_in[k], 16)

                with sp.Fori(0, NSUP // BODY) as it:
                    for u in range(BODY):
                        load_bases_input(it * BODY + u, u % 2, it * BODY + u + 1)
                        load_silu(it * BODY + u, u % 2)
                load_silu(NSUP, 0)

            @block.gpsimd
            def _(pool):
                g_ = nc.gpsimd
                for t, value in ((si0, 0.0), (xr, 0.0), (B, 0.0), (wsp, 0.0), (wba, 0.0)):
                    g_.memset(t[:], value).then_inc(cleared, 1)
                g_.memset(ends[:, 0:1], 2.0).then_inc(cleared, 1)
                g_.memset(ends[:, 1:2], 1.0).then_inc(cleared, 1)

                def store(g, k):
                    pool.wait_ge(o_done, g + 3)
                    for j in range(NSUB):
                        pool.dma_start(oq[:, bass.ds(g * SUP + j * SUB, SUB)], O[32 * j:32 * j + C, k, :]).then_inc(stored[k], 16)

                with pool.Fori(0, NSUP // BODY) as it:
                    for u in range(BODY):
                        store(it * BODY + u, u % 2)
                store(NSUP, 0)
                pool.wait_ge(stored[0], (NSUP // 2 + 1) * STORE)
                pool.wait_ge(stored[1], NSUP // 2 * STORE)
                for n in range(NB):
                    src = oq[:, SUP + n * IMG + PW:SUP + n * IMG + PW + H * PW].rearrange("c (h w) -> c h w", w=PW)[:, :, 1:1 + W]
                    pool.dma_start(out[n], src).then_inc(out_stored, 16)
                pool.wait_ge(out_stored, NB * 16)

            @block.scalar
            def _(act):
                s_ = nc.scalar
                act.sem_inc(b_done, 2)
                act.wait_ge(w_in, 80)
                act.wait_ge(cleared, 7)
                with act.Fori(0, NSUP // BODY) as it:
                    for u in range(BODY):
                        g = it * BODY + u
                        x = gx[:, u % 2, :]
                        act.wait_ge(gx_in[u % 2], (it * (BODY // 2) + u // 2 + 1) * (SPLINE * 16))
                        s_.activation(x, x, ACT.Abs, bias=place[:], scale=1.0 / GRID_STEP).then_inc(v_done, 1)
                        act.wait_ge(v_done, g + 1)
                        act.wait_ge(cube_a, g)
                        s_.activation(a[:], x, ACT.Relu, bias=ends[:, 0:1], scale=-1.0).then_inc(a_done, 1)
                        act.wait_ge(cube_b, g)
                        s_.activation(b[:], x, ACT.Relu, bias=ends[:, 1:2], scale=-1.0).then_inc(b_done, 1)
                        act.wait_ge(a_done, g + 1)
                        act.wait_ge(bases, g)
                        s_.activation(a2[:], a[:], ACT.Square).then_inc(a2_done, 1)
                        act.wait_ge(b_done, g + 1 + 2)
                        s_.activation(b2[:], b[:], ACT.Square).then_inc(b2_done, 1)

            @block.vector
            def _(dve):
                v = nc.vector
                link = Chain(dve, wchain)
                dve.sem_inc(o_done, 2)
                dve.wait_ge(w_in, 80)
                dve.wait_ge(cleared, 7)
                link(v.tensor_tensor(sw[:], sw[:], scaler[:], ALU.mult))
                link(v.tensor_reduce(scaler[:, 0, :, :], sw[:].rearrange("p m n f -> p n f m"), AX.X, ALU.add))
                link(v.tensor_scalar(wsp[:, :, 0:C], scaler[:, 0, :, :], 1.0 / 6, None, ALU.mult))
                v.tensor_reduce(wba[:, :, 0:C], bw[:].rearrange("p k m f -> p k f m"), AX.X, ALU.add).then_inc(w_ready, 1)

                def finish(g, k, before):
                    dve.wait_ge(o_made, g + 1 + 4)
                    dve.wait_ge(stored[k], before * STORE)
                    v.scalar_tensor_tensor(O[:, k, :], ops[:, k, 0:SUB], cbias[:], xr[:, k, :],
                                           ALU.add, ALU.add).then_inc(o_done, 1)

                with dve.Fori(0, NSUP // BODY) as it:
                    for u in range(BODY):
                        g = it * BODY + u
                        dve.wait_ge(a2_done, g + 1)
                        v.tensor_tensor(a2[:], a2[:], a[:], ALU.mult).then_inc(cube_a, 1)
                        dve.wait_ge(b2_done, g + 1)
                        v.scalar_tensor_tensor(b2[:], b2[:], -4.0, b[:], ALU.mult, ALU.mult).then_inc(cube_b, 1)
                        dve.wait_ge(cube_b, g + 1)
                        dve.wait_ge(o_made, g + 1)
                        v.tensor_tensor(B[:, u, :], a2[:], b2[:], ALU.add).then_inc(bases, 1)
                        if u:
                            finish(g - 1, (u - 1) % 2, it * (BODY // 2) + (u - 1) // 2)
                    finish(it * BODY + BODY - 1, (BODY - 1) % 2, it * (BODY // 2) + (BODY - 1) // 2)
                finish(NSUP, 0, NSUP // 2)

            @block.tensor
            def _(pe):
                t = nc.tensor
                pe.sem_inc(o_made, 4)
                pe.wait_ge(w_ready, 1)

                def convolve(slot, k):
                    bank = ops[:, k, :]
                    for n, (w, x) in enumerate(((wba[:, 0, :], si), (wba[:, 1, :], si0))):
                        for j in range(NSUB):
                            t.matmul(bank[32 * j:32 * j + 32, 0:SUB], w, x[:, k, j * SUB:(j + 1) * SUB],
                                     start=n == 0, stop=False, skip_group_check=True)
                    for p in range(9):
                        for j in range(NSUB):
                            at = 0
                            while at < SUB:
                                src = j * SUB + OFFS[p] + at
                                where, src = src // SUP, src % SUP
                                n = min(SUB - at, SUP - src)
                                last = t.matmul(bank[32 * j:32 * j + 32, at:at + n], wsp[:, p, :],
                                                B[:, (slot + where) % BODY, src:src + n],
                                                start=False, stop=p == 8, skip_group_check=True)
                                at += n
                    last.then_inc(o_made, 1)

                with pe.Fori(0, NSUP // BODY) as it:
                    for u in range(BODY):
                        g = it * BODY + u
                        pe.wait_ge(bases, g + 1)
                        pe.wait_ge(si_in[u % 2], (it * (BODY // 2) + u // 2 + 1) * (13 * 16))
                        pe.wait_ge(o_done, g + 1)
                        convolve((u - 1) % BODY, u % 2)
                pe.wait_ge(si_in[0], (NSUP // 2 + 1) * (13 * 16))
                pe.wait_ge(o_done, NSUP + 1)
                convolve(BODY - 1, 0)


def build(nc, io, stages=(0, 1, 2, 3)):
    nc.disable_value_cache = True

    def dram(name, shape, dt=F32):
        return nc.dram_tensor(name, shape, dt, kind="Internal").ap()

    x1 = dram("x1", (P, HW))
    x2 = dram("x2", (P, HW))
    pw = dram("pw", (3, C, DEG, LINE), BF16)
    out2 = dram("out2", (C, SUP + LINE))
    x3q = dram("x3q", (C, SUP + LINE))
    g3q = dram("g3q", (C, LINE))
    s3q = dram("s3q", (C, MARGIN + SUP + LINE + MARGIN))
    oq = dram("oq", (C, SUP + LINE))
    x = io["x"].rearrange("b c h w -> (b c) (h w)")
    if 0 in stages:
        g0 = dram("g0", (P, H, W + 2))
        norm0(nc, x, io["pair"], g0)
        layer0(nc, io, g0, x1)
    if 1 in stages:
        layer1(nc, x1 if 0 in stages else x, x2, pw, io["pair"], (io["w1_mats"], io["w1_vecs"]))
    if 2 in stages:
        layer2(nc, pw, (io["w2_p"], io["w2_q"], io["w2_mask"], io["w2_sums"], io["w2_pick"]), out2)
    if 3 in stages:
        layer3(nc, x2, out2, io["pair"],
               (io["w3_spline"], io["w3_scaler"], io["w3_base"], io["w3_place"], io["w3_bias"]),
               x3q, g3q, s3q, oq, io["out"])


def lay_out(inputs):
    import numpy as np

    def diagonal(m, times):
        rows, cols = m.shape
        full = np.zeros((times * rows, times * cols), m.dtype)
        for k in range(times):
            full[k * rows:(k + 1) * rows, k * cols:(k + 1) * cols] = m
        return full

    a = {k: np.ascontiguousarray(v) for k, v in inputs.items()}
    f32 = np.float32
    got = {"x": a["x"]}
    got["pair"] = diagonal(np.full((2, 2), 0.5, f32), P // 2)
    wa = a["L0_conv_w_attn"]
    order = np.array([c * 3 + i for i in range(3) for c in range(C)])
    qkv = np.zeros((2, 48, 3, 2, 48), f32)
    for s in range(2):
        for k in range(3):
            qkv[s, :, k, s, :] = wa[k * 48:(k + 1) * 48][:, order].T
    got["w0_qkv"] = qkv.reshape(96, 288)
    got["w0_proj"] = diagonal(a["L0_conv_w_attn_proj"][order], 2)
    fc = np.zeros((2, 48, 2, 192), f32)
    for s in range(2):
        fc[s, :, s, :] = a["L0_conv_w_fc"][:, order].T
    got["w0_fc"] = fc.reshape(96, 384)
    got["w0_fc_proj"] = diagonal(a["L0_conv_w_fc_proj"][order], 2)
    got["w0_conv"] = diagonal(a["L0_conv_conv_w"][:, order].T, 2)
    got["w0_bias"] = np.ascontiguousarray(np.broadcast_to(np.tile(a["L0_conv_conv_b"], 2), (P, 2 * C)))
    got["ident"] = np.eye(P, dtype=f32)
    got["w0_center"] = diagonal((np.eye(48) - 1.0 / 48).astype(f32), 2)
    got["w1_mats"] = np.ascontiguousarray(np.stack(
        [diagonal(a["L1_conv_" + n], NB) for n in ("Wc", "W1")]
        + [diagonal(a["L1_conv_" + n].T, NB) for n in ("W2", "W3", "W4")], axis=1))
    got["w1_vecs"] = np.ascontiguousarray(np.stack([np.tile(a["L1_conv_" + n], NB) for n in ("bc", "b1", "b2", "b3", "b4")], axis=1))
    for name, src in (("w2_p", a["L2_conv_A"]), ("w2_q", a["L2_conv_Bc"])):
        full = np.zeros((C, C, 9, DEG + 1), f32)
        full[..., :DEG + 1 if name == "w2_p" else 0] = src if name == "w2_p" else 0
        if name == "w2_q":
            full[..., 1:1 + src.shape[-1]] = src
        paired = np.zeros((KROWS, NCG, NPP, CG, 2, C), f32)
        centre = np.zeros((KROWS, NCG, 8, C), f32)
        for cg in range(NCG):
            for c in range(CG):
                w = full[:, cg * CG + c]
                for j in range(len(X_PARTS)):
                    rows = slice(j * CG * DEG + c * DEG, j * CG * DEG + (c + 1) * DEG)
                    for k, p in enumerate(AROUND):
                        paired[rows, cg, k // 2, c, k % 2, :] = w[:, p, 1:].T
                    centre[rows, cg, (cg % 2) * CG + c, :] = w[:, CENTER, 1:].T
                for k, p in enumerate(AROUND):
                    paired[-3:, cg, k // 2, c, k % 2, :] = w[:, p, 0]
                centre[-3:, cg, (cg % 2) * CG + c, :] = w[:, CENTER, 0]
        got[name] = np.ascontiguousarray(np.concatenate([paired.reshape(KROWS, -1), centre.reshape(KROWS, -1)], axis=1))
    mask = np.zeros((KROWS, 3), f32)
    for j, part in enumerate(A_PARTS):
        mask[j * CG * DEG:(j + 1) * CG * DEG, part] = 1
    mask[-3:] = np.eye(3)
    got["w2_mask"] = mask
    sums = np.zeros((P, 2, 32), f32)
    sums[np.arange(P), 0, np.arange(P) % 32] = 1
    sums[np.arange(P), 1, np.arange(P) % C] = 1
    got["w2_sums"] = sums
    pick = np.zeros((P, len(AROUND), 32), f32)
    pick[np.arange(P), np.arange(P) // C, np.arange(P) % C] = 1
    got["w2_pick"] = pick
    sw = a["L3_conv_spline_weight"].transpose(4, 1, 2, 3, 0)
    got["w3_spline"] = np.ascontiguousarray(sw.reshape(P, 9, 9, C))
    sc = a["L3_conv_spline_scaler"].transpose(1, 2, 3, 0)
    got["w3_scaler"] = np.ascontiguousarray(np.broadcast_to(sc, (SPLINE,) + sc.shape).reshape(P, 9, 9, C))
    bw = a["L3_conv_base_weight"].transpose(3, 1, 2, 0)
    base = np.zeros((P, 2, 9, C), f32)
    base[:, 0] = bw[AROUND].reshape(P, 9, C)
    base[:C, 1] = bw[CENTER]
    got["w3_base"] = base
    got["w3_place"] = np.repeat(3.5 - np.arange(SPLINE), C).astype(f32).reshape(P, 1)
    bias = np.zeros((4, 32), f32)
    bias[:, :C] = a["L3_conv_bias_weight"]
    got["w3_bias"] = bias.reshape(P, 1)
    return got


def kernel(**inputs):
    import numpy as np
    import concourse.bacc as bacc
    from concourse.bass_utils import run_bass_kernel_spmd

    nc = bacc.Bacc("TRN2", target_bir_lowering=False, num_devices=1)
    arrays = lay_out(inputs)
    io = {k: nc.dram_tensor(f"in_{k}", v.shape, mybir.dt.from_np(v.dtype), kind="ExternalInput").ap() for k, v in arrays.items()}
    io["out"] = nc.dram_tensor("out_x", (NB, C, H, W), F32, kind="ExternalOutput").ap()
    build(nc, io)
    r = run_bass_kernel_spmd(nc, [{f"in_{k}": v for k, v in arrays.items()}], core_ids=[0])
    return r.results[0]["out_x"]
```

```python
import concourse.bass as bass
from concourse import mybir
from contextlib import ExitStack

F32 = mybir.dt.float32
BF16 = mybir.dt.bfloat16
I32 = mybir.dt.int32
ALU = mybir.AluOpType
ACT = mybir.ActivationFunctionType
AX = mybir.AxisListType

P = 128
NB, C, H, W = 8, 16, 128, 128
HW = H * W
GN_EPS = 1e-5

PW = W + 1
SUB = 509
IMG = 33 * SUB
LINE = NB * IMG
NSUB = 4
SUP = NSUB * SUB
NSUP = LINE // SUP
SLOTS = 3
assert IMG >= (H + 2) * PW + 1 and NSUP * SUP == LINE and NSUP % SLOTS == 0
OFFS = [dy * PW + dx for dy in (-1, 0, 1) for dx in (-1, 0, 1)]
CENTER = 4
AROUND = [n for n in range(9) if n != CENTER]
MARGIN = 256
assert MARGIN >= max(OFFS)

X_PARTS = [0, 0, 0, 1, 1, 2]
A_PARTS = [0, 1, 2, 0, 1, 0]
DEG = 5
CG = 4
NCG = C // CG
KROWS = len(X_PARTS) * CG * DEG + 3
assert KROWS <= P

def image_rows(t):
    return t[:, PW:PW + H * PW].rearrange("p (h w) -> p h w", w=PW)[:, :, 1:1 + W]

class Chain:

    def __init__(self, engine, sem):
        self.engine, self.sem, self.n = engine, sem, 0

    def __call__(self, instruction):
        self.n += 1
        instruction.then_inc(self.sem, 1)
        self.engine.wait_ge(self.sem, self.n)

class Norm:

    CHUNKS = 32

    def __init__(self, nc, ctx, tag):
        def sb(name, shape):
            return ctx.enter_context(nc.sbuf_tensor(f"{tag}_{name}", shape, F32))

        self.nc = nc
        self.stats = sb("stats", [P, self.CHUNKS, 6])
        self.own = sb("own", [P, 2])
        self.dev = sb("dev", [P, 2])
        self.spread = sb("spread", [P, 1])
        self.mean = sb("mean", [P, 1])
        self.std = sb("std", [P, 1])
        self.rstd = sb("rstd", [P, 1])
        self.shift = sb("shift", [P, 1])
        self.eps = sb("eps", [P, 1])
        self.pair = sb("pair", [P, P])
        self.sums = ctx.enter_context(nc.psum_tensor(f"{tag}_sums", [P, 2], F32))
        self.pair_in = ctx.enter_context(nc.semaphore(f"{tag}_pair_in"))
        self.own_ready = ctx.enter_context(nc.semaphore(f"{tag}_own_ready"))
        self.mean_ready = ctx.enter_context(nc.semaphore(f"{tag}_mean_ready"))
        self.spread_ready = ctx.enter_context(nc.semaphore(f"{tag}_spread_ready"))
        self.var_ready = ctx.enter_context(nc.semaphore(f"{tag}_var_ready"))
        self.std_ready = ctx.enter_context(nc.semaphore(f"{tag}_std_ready"))

    def sync_part(self, sp, pair_dram):
        sp.dma_start(self.pair[:], pair_dram).then_inc(self.pair_in, 16)

    def vector_part(self, dve, link, x, chunk_in):
        v = self.nc.vector
        v.memset(self.eps[:], GN_EPS)
        n = HW // self.CHUNKS
        for k in range(self.CHUNKS):
            chunk_in(dve, k)
            last = v.bn_stats(self.stats[:, k, :], x(k, n))
        link(last)
        link(v.bn_aggr(self.own[:], self.stats[:].rearrange("p k s -> p (k s)")))
        link(v.tensor_copy(self.spread[:], self.own[:, 0:1]))
        v.tensor_copy(self.mean[:], self.own[:, 0:1]).then_inc(self.own_ready, 1)
        dve.wait_ge(self.mean_ready, 1)
        link(v.tensor_copy(self.mean[:], self.sums[:, 0:1]))
        link(v.tensor_tensor(self.dev[:, 0:1], self.own[:, 0:1], self.mean[:], ALU.subtract))
        link(v.tensor_tensor(self.dev[:, 1:2], self.dev[:, 0:1], self.dev[:, 0:1], ALU.mult))
        v.tensor_tensor(self.spread[:], self.own[:, 1:2], self.dev[:, 1:2],
                        ALU.add).then_inc(self.spread_ready, 1)
        dve.wait_ge(self.std_ready, 1)
        link(v.reciprocal(self.rstd[:], self.std[:]))
        link(v.scalar_tensor_tensor(self.shift[:], self.mean[:], -1.0, self.rstd[:], ALU.mult, ALU.mult))

    def tensor_part(self, pe):
        t = self.nc.tensor
        pe.wait_ge(self.pair_in, 16)
        pe.wait_ge(self.own_ready, 1)
        t.matmul(self.sums[:, 0:1], self.pair[:], self.own[:, 0:1], start=True, stop=True).then_inc(self.mean_ready, 1)
        pe.wait_ge(self.spread_ready, 1)
        t.matmul(self.sums[:, 1:2], self.pair[:], self.spread[:], start=True, stop=True).then_inc(self.var_ready, 1)

    def scalar_part(self, act):
        act.wait_ge(self.var_ready, 1)
        self.nc.scalar.activation(self.std[:], self.sums[:, 1:2], ACT.Sqrt, bias=self.eps[:]).then_inc(self.std_ready, 1)

EMB = 3 * C
SETS = 2
F2 = SETS * EMB
HEADS, HEAD = 4, 12
SH = SETS * HEADS
CW = 8
TW = CW + 2
NCHUNK = W // CW
NPAIR = NB // SETS
HID = 4 * EMB
LN_EPS = 1e-5
GELUS_BEFORE_EXP = 3
QKV_BEFORE_STD = 3, 9
T_GROUPS = {"norm2": (6, "mlp"), "norm3": (2, "out"), "mix": (6, "attn"), "norm1": (4, "ahead")}
T_WIDTHS = (3, 3, 2, 2)
C_GROUPS = {"conv": (2, "out"), "mlp": (6, "mlp"), "proj": (6, "attn")}

class Plan:

    def __init__(self, pair, t, kind, parity):
        self.first, self.attn, self.ahead, self.mlp, self.out = kind
        self.pair, self.parity = pair, parity
        self.t = t
        self.chunk = pair * NCHUNK + t
        self.behind = pair * NCHUNK + t - 1
        self.last = pair * NCHUNK + t - 2
        self.t_base, self.t_at = self.ring(T_GROUPS)
        self.c_base, self.c_at = self.ring(C_GROUPS)

    def ring(self, groups):
        stage = {"ahead": -1, "attn": 0, "mlp": 1, "out": 2}
        sizes = {k: sum(n for n, of in groups.values() if stage[of] == k) for k in range(-1, 3)}
        total = sum(sizes.values())
        if self.first:
            before = 0
        elif isinstance(self.t, int):
            before = sum(size * min(NCHUNK, max(0, self.t - k)) for k, size in sizes.items())
        else:
            before = self.t * total - sum(k * size for k, size in sizes.items())
        at, n = {"first": 0}, sizes[-1] if self.first else 0
        for name, (size, of) in groups.items():
            if {"ahead": self.ahead, "attn": self.attn, "mlp": self.mlp, "out": self.out}[of]:
                at[name], n = n, n + size
        return self.pair * (NCHUNK * total) + before, at

def steps(engine, body):
    def kind(t):
        return t == 0, t < NCHUNK, t + 1 < NCHUNK, 1 <= t <= NCHUNK, t >= 2

    def peeled(pair, t):
        body(Plan(pair, t, kind(t), t % 2))

    with engine.Fori(0, NPAIR) as pair:
        peeled(pair, 0)
        peeled(pair, 1)
        with engine.Fori(1, NCHUNK // 2 - 1) as twice:
            for odd in range(2):
                body(Plan(pair, twice * 2 + odd, kind(2), odd))
        for t in range(NCHUNK - 2, NCHUNK + 2):
            peeled(pair, t)

def norm0(nc, x, pair, g0):
    ROWS = 32
    with ExitStack() as ctx:
        def sb(name, shape, dt=F32):
            return ctx.enter_context(nc.sbuf_tensor(name, shape, dt))

        def sem(name):
            return ctx.enter_context(nc.semaphore(name))

        norm = Norm(nc, ctx, "n0")
        X = sb("n0_x", [P, HW])
        G = sb("n0_g", [P, H, W + 2])
        x_in = [sem(f"n0_x_in{k}") for k in range(8)]
        chain, ready, stored = sem("n0_chain"), sem("n0_ready"), sem("n0_stored")
        with nc.Block() as block:
            @block.sync
            def _(sp):
                for k in range(8):
                    sp.dma_start(X[:, k * HW // 8:(k + 1) * HW // 8], x[:, k * HW // 8:(k + 1) * HW // 8]).then_inc(x_in[k], 16)
                norm.sync_part(sp, pair)
                for k in range(H // ROWS):
                    sp.wait_ge(ready, 3 * (k + 1))
                    sp.dma_start(g0[:, k * ROWS:(k + 1) * ROWS, :], G[:, k * ROWS:(k + 1) * ROWS, :]).then_inc(stored, 16)
                sp.wait_ge(stored, H // ROWS * 16)

            @block.vector
            def _(dve):
                v = nc.vector
                link = Chain(dve, chain)
                norm.vector_part(dve, link, lambda k, n: X[:, k * n:(k + 1) * n],
                                 lambda e, k: e.wait_ge(x_in[k // 4], 16))
                x3 = X[:].rearrange("p (h w) -> p h w", w=W)
                for k in range(H // ROWS):
                    r = slice(k * ROWS, (k + 1) * ROWS)
                    for to, of in ((slice(1, W + 1), slice(0, W)), (slice(0, 1), slice(W - 1, W)), (slice(W + 1, W + 2), slice(0, 1))):
                        v.tensor_scalar(G[:, r, to], x3[:, r, of], norm.rstd[:], norm.shift[:], ALU.mult, ALU.add).then_inc(ready, 1)

            @block.tensor
            def _(pe):
                norm.tensor_part(pe)

            @block.scalar
            def _(act):
                norm.scalar_part(act)

def layer0(nc, io, g0, x1):
    with ExitStack() as ctx:
        def sb(name, shape, dt=F32):
            return ctx.enter_context(nc.sbuf_tensor(name, shape, dt))

        def ps(name, shape):
            return ctx.enter_context(nc.psum_tensor(name, shape, F32))

        def sem(name):
            return ctx.enter_context(nc.semaphore(name))

        ident = sb("a_ident", [P, P])
        wqkv = sb("a_wqkv", [F2, 3 * F2])
        wproj = sb("a_wproj", [F2, F2])
        wfc = sb("a_wfc", [F2, SETS * HID])
        wfp = sb("a_wfp", [P, 3, F2])
        wconv = sb("a_wconv", [F2, SETS * C])
        cbias = sb("a_cbias", [P, SETS * C])
        raw = sb("a_raw", [F2, F2 + SETS * HID + F2])
        eps = sb("a_eps", [P, 1])
        TB = sb("a_tb", [P, F2, W + 2])
        XB = sb("a_xb", [P, SETS * C, W])
        Tc = sb("a_tc", [P, 2, TW, F2])
        hA = sb("a_ha", [P, TW, F2])
        hAT = sb("a_hat", [F2, TW, P])
        QKV = sb("a_qkv", [P, TW, 3 * F2])
        PR = sb("a_pr", [P, 9, CW * F2])
        Sc = sb("a_sc", [P, 5, TW, SH])
        At = sb("a_at", [P, 3, 3, CW * SH])
        yT = sb("a_yt", [F2, 3, CW, P])
        x1c = sb("a_x1c", [P, 3, CW, F2])
        hB = sb("a_hb", [P, 3, CW, F2])
        hBT = sb("a_hbt", [F2, 3 * CW, P])
        G = sb("a_g", [P, 2, 3, 512])
        x2c = sb("a_x2c", [P, 3, CW, F2])
        zs = sb("a_zs", [P, CW, F2])
        zT = sb("a_zt", [F2, CW, P])
        st = sb("a_st", [P, 8, 3 * CW * SETS])
        sm = sb("a_sm", [P, 3, 3 * CW * SH])
        tps = ps("a_tps", [P, 2, 512])
        qps = ps("a_qps", [P, 2, 512])
        fps = ps("a_fps", [P, 2, 512])
        cps = ps("a_cps", [P, 2, 512])

        w_in, cent_made, w_ready = sem("a_w_in"), sem("a_cent_made"), sem("a_w_ready")
        tb_in, xb_in, xb_ready, stored = sem("a_tb_in"), sem("a_xb_in"), sem("a_xb_ready"), sem("a_stored")
        n1 = sem("a_n1")
        n1_sq, n1_r = sem("a_n1_sq"), sem("a_n1_r")
        sc_v, sc_p = sem("a_sc_v"), sem("a_sc_p")
        soft, soft_exp = sem("a_soft"), sem("a_soft_exp")
        val_v, val_p = sem("a_val_v"), sem("a_val_p")
        n2, n2_sq, n2_r = sem("a_n2"), sem("a_n2_sq"), sem("a_n2_r")
        n3, n3_sq, n3_r = sem("a_n3"), sem("a_n3_sq"), sem("a_n3_r")
        t_made, t_read = sem("a_t_made"), sem("a_t_read")
        q_made, q_read = sem("a_q_made"), sem("a_q_read")
        f_made, f_read = sem("a_f_made"), sem("a_f_read")
        c_made, c_read = sem("a_c_made"), sem("a_c_read")
        CPP = NCHUNK * sum(n for n, _ in C_GROUPS.values())

        with nc.Block() as block:
            def x1v(pair, s):
                n = pair * SETS + s
                return x1[n * C:(n + 1) * C].rearrange("c (h w) -> h c w", w=W)

            @block.sync
            def _(sp):
                for t, src in ((ident, io["ident"]), (wqkv, io["w0_qkv"]), (wfc, io["w0_fc"]), (wconv, io["w0_conv"]),
                               (cbias, io["w0_bias"])):
                    sp.dma_start(t[:], src).then_inc(w_in, 16)
                at = 0
                for src, n in ((io["w0_proj"], F2), (io["w0_fc_proj"], SETS * HID), (io["w0_center"], F2)):
                    sp.dma_start(raw[:, at:at + n], src).then_inc(w_in, 16)
                    at += n
                for pair in range(NPAIR):
                    if pair:
                        sp.wait_ge(n1, pair * NCHUNK * 5)
                    for s in range(SETS):
                        rows = g0[(pair * SETS + s) * C:(pair * SETS + s + 1) * C]
                        for i in range(3):
                            to = TB[:, s * EMB + i * C:s * EMB + (i + 1) * C, :]
                            lo, hi = max(0, 1 - i), min(H, H + 1 - i)
                            sp.dma_start(to[lo:hi], rows[:, lo + i - 1:hi + i - 1, :].rearrange("c h w -> h c w")).then_inc(tb_in, 16)
                            if i != 1:
                                edge, of = (0, H - 1) if i == 0 else (H - 1, 0)
                                sp.dma_start(to[edge:edge + 1], rows[:, of:of + 1, :].rearrange("c h w -> h c w")).then_inc(tb_in, 16)
                    if pair:
                        sp.wait_ge(c_read, pair * CPP + 2)
                        for s in range(SETS):
                            sp.dma_start(x1v(pair - 1, s), XB[:, s * C:(s + 1) * C, :]).then_inc(stored, 16)
                        sp.wait_ge(stored, pair * SETS * 16)
                    for s in range(SETS):
                        sp.dma_start(XB[:, s * C:(s + 1) * C, :],
                                     io["x"][pair * SETS + s].rearrange("c h w -> h c w")).then_inc(xb_in, 16)
                sp.wait_ge(c_read, NPAIR * CPP + 2)
                for s in range(SETS):
                    sp.dma_start(x1v(NPAIR - 1, s), XB[:, s * C:(s + 1) * C, :]).then_inc(stored, 16)
                sp.wait_ge(stored, NPAIR * SETS * 16)

            @block.tensor
            def _(pe):
                t_ = nc.tensor
                pe.wait_ge(w_in, 8 * 16)
                center = raw[:, F2 + SETS * HID:]
                t_.matmul(cps[0:F2, 0, 0:F2], raw[:, 0:F2], center, start=True, stop=True)
                for m in range(3):
                    last = t_.matmul(cps[:, 1, m * F2:(m + 1) * F2], raw[:, F2 + m * P:F2 + (m + 1) * P], center,
                                     start=True, stop=True)
                last.then_inc(cent_made, 1)
                pe.wait_ge(w_ready, 2)

                def transposes(src, first, n, base, k):
                    pe.wait_ge(t_read, base + k + 1)
                    for j in range(n):
                        last = t_.transpose(tps[0:F2, k % 2, j * P:(j + 1) * P], src[:, first + j, :], ident[:])
                    last.then_inc(t_made, 1)

                def tokens(base, g, first=0):
                    transposes(hA, sum(T_WIDTHS[:g]), T_WIDTHS[g], base, first + g)

                def body(p):
                    if p.attn:
                        k = p.chunk
                        if p.first:
                            pe.wait_ge(n1, k * 5 + 5)
                            for g in range(len(T_WIDTHS)):
                                tokens(p.t_base, g)
                        pe.wait_ge(t_read, p.t_base + (len(T_WIDTHS) if p.first else 0) + 2)
                        for w in range(TW):
                            pe.wait_ge(q_read, k * TW + w + 1)
                            t_.matmul(qps[:, w % 2, 0:3 * F2], hAT[:, w, :], wqkv[:], start=True, stop=True).then_inc(q_made, 1)
                    if p.mlp:
                        kb = p.behind
                        for g in range(6):
                            pe.wait_ge(n2, kb * 6 + 3 + g // 2 + 1)
                            transposes(hB[:].rearrange("p t w f -> p (t w) f"), g * 4, 4, p.t_base, p.t_at["norm2"] + g)
                        if not p.out:
                            hidden(p, kb, 0)
                    if p.out:
                        pe.wait_ge(n3, p.last * 4 + 4)
                        for g in range(2):
                            transposes(zs, g * 4, 4, p.t_base, p.t_at["norm3"] + g)
                        if p.mlp:
                            hidden(p, kb, 0)
                        for g in range(2):
                            pe.wait_ge(t_read, p.t_base + p.t_at["norm3"] + g + 1 + 2)
                            c = p.c_at["conv"] + g
                            pe.wait_ge(c_read, p.c_base + c + 1)
                            for j in range(4):
                                last = t_.matmul(cps[:, c % 2, j * 32:(j + 1) * 32], zT[:, g * 4 + j, :], wconv[:],
                                                 start=True, stop=True)
                            last.then_inc(c_made, 1)
                    if p.mlp:
                        for g in range(6):
                            if g < 5:
                                hidden(p, kb, g + 1)
                            pe.wait_ge(f_read, kb * 18 + g * 3 + 3 + 2)
                            c = p.c_at["mlp"] + g
                            pe.wait_ge(c_read, p.c_base + c + 1)
                            for j in range(4):
                                for m, lo, hi in ((1, 0, F2), (0, 0, EMB), (2, EMB, F2)):
                                    last = t_.matmul(cps[:, c % 2, j * F2 + lo:j * F2 + hi], G[:, g % 2, m, j * P:(j + 1) * P],
                                                     wfp[:, m, lo:hi], start=m == 1, stop=m == 2, skip_group_check=True)
                            last.then_inc(c_made, 1)
                    if p.attn:
                        k = p.chunk
                        for d in range(3):
                            pe.wait_ge(val_p, k * 6 + 2 * d + 2)
                            for half in range(2):
                                transposes(PR[:, 3 * d, :].rearrange("p (w f) -> p w f", f=F2), half * 4, 4,
                                           p.t_base, p.t_at["mix"] + 2 * d + half)
                        for g in range(6):
                            pe.wait_ge(t_read, p.t_base + p.t_at["mix"] + g + 1 + 2)
                            c = p.c_at["proj"] + g
                            pe.wait_ge(c_read, p.c_base + c + 1)
                            for j in range(4):
                                last = t_.matmul(cps[:, c % 2, j * F2:(j + 1) * F2], yT[:, g // 2, (g % 2) * 4 + j, :], wproj[:],
                                                 start=True, stop=True)
                            last.then_inc(c_made, 1)
                            if p.ahead and g < len(T_WIDTHS):
                                if g == 0:
                                    pe.wait_ge(n1, (k + 1) * 5 + 5)
                                tokens(p.t_base, g, p.t_at["norm1"])

                def hidden(p, kb, g):
                    pe.wait_ge(t_read, p.t_base + p.t_at["norm2"] + g + 1 + 2)
                    for m in range(3):
                        n = g * 3 + m
                        pe.wait_ge(f_read, kb * 18 + n + 1)
                        t_.matmul(fps[:, n % 2, :], wfc[:, m * P:(m + 1) * P],
                                  hBT[:, g * 4:(g + 1) * 4, :].rearrange("f w h -> f (w h)"), start=True, stop=True).then_inc(f_made, 1)

                steps(pe, body)

            def squares():
                n = TW * F2
                return PR[:].rearrange("p k n -> p (k n)")[:, n:n + 3 * CW * F2].rearrange("p (n f) -> p n f", f=F2)

            def scratch(d):
                n = TW * F2
                return PR[:].rearrange("p k n -> p (k n)")[:, (d + 2) * n:(d + 3) * n].rearrange("p (w f) -> p w f", f=F2)

            def query_key(engine, d):
                lo, m = max(0, -d), TW - abs(d)
                return engine.tensor_tensor(scratch(d)[:, 0:m, :], QKV[:, lo:lo + m, 0:F2],
                                            QKV[:, lo + d:lo + d + m, F2:2 * F2], ALU.mult)

            @block.vector
            def _(dve):
                v = nc.vector
                dve.sem_inc(c_read, 2)
                dve.sem_inc(val_v, 9)
                v.memset(eps[:], LN_EPS).then_inc(w_ready, 1)
                dve.wait_ge(cent_made, 1)
                v.tensor_copy(wproj[:], cps[0:F2, 0, 0:F2])
                v.tensor_copy(wfp[:].rearrange("p m f -> p (m f)"), cps[:, 1, 0:3 * F2]).then_inc(w_ready, 1)
                dve.wait_ge(w_ready, 2)

                def own(sem_, base, instruction, i):
                    instruction.then_inc(sem_, 1)
                    dve.wait_ge(sem_, base + i)

                def center_tokens(k, parity, w0):
                    b = k * 5
                    tok = TB[:, :, bass.ds(w0, TW)]
                    total, mean = (st[:, n, 0:TW * SETS] for n in range(2))
                    own(n1, b, v.tensor_reduce(total.rearrange("p (w s) -> p w s", s=SETS),
                                               tok.rearrange("p (s f) w -> p w s f", s=SETS), AX.X, ALU.add), 1)
                    own(n1, b, v.tensor_scalar(mean, total, 1.0 / EMB, None, ALU.mult), 2)
                    v.tensor_tensor(Tc[:, parity].rearrange("p w (s f) -> p w s f", s=SETS),
                                    tok.rearrange("p (s f) w -> p w s f", s=SETS),
                                    mean.rearrange("p (w s) -> p w s", s=SETS).unsqueeze(3).broadcast_to([P, TW, SETS, EMB]),
                                    ALU.subtract).then_inc(n1, 1)

                def sum_tokens(k):
                    dve.wait_ge(n1_sq, k + 1)
                    v.tensor_reduce(st[:, 2, 0:TW * SETS], hA[:].rearrange("p w (s f) -> p (w s) f", s=SETS),
                                    AX.X, ALU.add).then_inc(n1, 1)

                def scale_tokens(k, parity):
                    dve.wait_ge(n1_r, k + 1)
                    v.tensor_tensor(hA[:].rearrange("p w (s f) -> p (w s) f", s=SETS),
                                    Tc[:, parity].rearrange("p w (s f) -> p (w s) f", s=SETS),
                                    st[:, 3, 0:TW * SETS].unsqueeze(2).broadcast_to([P, TW * SETS, EMB]), ALU.mult).then_inc(n1, 1)

                def norm_residual(p):
                    k = p.chunk
                    for d in range(3):
                        if d == 1:
                            add_attention(p, 4)
                            add_attention(p, 5)
                        dve.wait_ge(n2_sq, k * 3 + d + 1)
                        v.tensor_reduce(st[:, 4, d * CW * SETS:(d + 1) * CW * SETS],
                                        hB[:, d].rearrange("p w (s f) -> p (w s) f", s=SETS), AX.X, ALU.add).then_inc(n2, 1)
                    dve.wait_ge(n2_r, k + 1)
                    for d in range(3):
                        v.tensor_tensor(hB[:, d].rearrange("p w (s f) -> p (w s) f", s=SETS),
                                        x1c[:, d].rearrange("p w (s f) -> p (w s) f", s=SETS),
                                        st[:, 5, d * CW * SETS:(d + 1) * CW * SETS].unsqueeze(2).broadcast_to([P, CW * SETS, EMB]),
                                        ALU.mult).then_inc(n2, 1)

                def norm_out(p):
                    b = p.last * 4
                    h3 = x2c[:].rearrange("p t w (s f) -> p (t w s) f", s=SETS)
                    dve.wait_ge(n3_sq, p.last * 3 + 3)
                    own(n3, b, v.tensor_reduce(st[:, 6, :], squares().rearrange("p n (s f) -> p (n s) f", s=SETS), AX.X, ALU.add), 1)
                    dve.wait_ge(n3_r, p.last + 1)
                    own(n3, b, v.tensor_tensor(h3, h3, st[:, 7, :].unsqueeze(2).broadcast_to([P, 3 * CW * SETS, EMB]), ALU.mult), 2)
                    dve.wait_ge(t_read, p.t_base + 2)
                    own(n3, b, v.tensor_tensor(zs[:], x2c[:, 0], x2c[:, 1], ALU.add), 3)
                    v.tensor_tensor(zs[:], zs[:], x2c[:, 2], ALU.add).then_inc(n3, 1)

                def scores(p):
                    k = p.chunk
                    dve.wait_ge(q_read, k * TW + TW + 2)
                    for n, d in enumerate((-1, 0, 1)):
                        query_key(nc.vector, d).then_inc(sc_v, 1)
                    for n, d in enumerate((-1, 0, 1, -2, 2)):
                        if n == 2 and p.out:
                            add_conv(p)
                        if n < 3:
                            dve.wait_ge(sc_v, k * 8 + n + 1)
                        else:
                            dve.wait_ge(sc_p, k * 2 + n - 2)
                        lo, m = max(0, -d), TW - abs(d)
                        v.tensor_reduce(Sc[:, d + 2, lo:lo + m, :],
                                        scratch(d)[:, 0:m, :].rearrange("p w (g e) -> p w g e", e=HEAD),
                                        AX.X, ALU.add).then_inc(sc_v, 1)
                    dve.wait_ge(sc_v, k * 8 + 8)

                def softmax_shift(p):
                    k, b = p.chunk, p.chunk * 9
                    top = sm[:, 0, :].rearrange("p (d n) -> p d n", d=3)
                    for d in range(3):
                        s = Sc[:, 2 - d:5 - d, d:d + CW, :].rearrange("p e w g -> p e (w g)")
                        own(soft, b, v.tensor_reduce(top[:, d, :], s.rearrange("p e n -> p n e"), AX.X, ALU.max), 2 * d + 1)
                        own(soft, b, v.tensor_tensor(At[:, d, :, :], s, top[:, d, :].unsqueeze(1).broadcast_to([P, 3, CW * SH]),
                                                     ALU.subtract), 2 * d + 2)

                def softmax_scale(p):
                    k, b = p.chunk, p.chunk * 9
                    dve.wait_ge(soft_exp, k + 1)
                    own(soft, b, v.tensor_reduce(sm[:, 1, :].rearrange("p (d n) -> p d n", d=3),
                                                 At[:].rearrange("p d e n -> p d n e"), AX.X, ALU.add), 7)
                    own(soft, b, v.reciprocal(sm[:, 2, :], sm[:, 1, :]), 8)
                    own(soft, b, v.tensor_tensor(At[:], At[:], sm[:, 2, :].rearrange("p (d n) -> p d n", d=3).unsqueeze(2)
                                                 .broadcast_to([P, 3, 3, CW * SH]), ALU.mult), 9)

                def values(p, d):
                    k = p.chunk
                    for e in range(3):
                        out = PR[:, 3 * d + e, :].rearrange("p (w g n) -> p w g n", g=SH, n=HEAD)
                        a = At[:, d, e, :].rearrange("p (w g) -> p w g", g=SH).unsqueeze(3).broadcast_to([P, CW, SH, HEAD])
                        val = QKV[:, e:e + CW, 2 * F2:3 * F2].rearrange("p w (g n) -> p w g n", n=HEAD)
                        v.tensor_tensor(out, val, a, ALU.mult).then_inc(val_v, 1)

                def add_attention(p, g):
                    c = p.c_at["proj"] + g
                    d, w = g // 2, (g % 2) * 4
                    dve.wait_ge(c_made, p.c_base + c + 1)
                    v.tensor_tensor(x1c[:, d, w:w + 4, :], cps[:, c % 2, 0:4 * F2].rearrange("p (w f) -> p w f", f=F2),
                                    Tc[:, p.parity, d + w:d + w + 4, :], ALU.add).then_inc(c_read, 1)

                def add_mlp(p, g):
                    c = p.c_at["mlp"] + g
                    d, w = g // 2, (g % 2) * 4
                    dve.wait_ge(c_made, p.c_base + c + 1)
                    v.tensor_tensor(x2c[:, d, w:w + 4, :], cps[:, c % 2, 0:4 * F2].rearrange("p (w f) -> p w f", f=F2),
                                    x1c[:, d, w:w + 4, :], ALU.add).then_inc(c_read, 1)

                def add_conv(p):
                    for g in range(2):
                        c = p.c_at["conv"] + g
                        dve.wait_ge(c_made, p.c_base + c + 1)
                        x = XB[:, :, bass.ds((p.t - 2) * CW + g * 4, 4)]
                        v.tensor_tensor(x, cps[:, c % 2, 0:P].rearrange("p (w o) -> p o w", w=4), x, ALU.add).then_inc(c_read, 1)

                def body(p):
                    if p.first:
                        dve.wait_ge(tb_in, p.pair * (10 * 16) + 10 * 16)
                        center_tokens(p.chunk, 0, 0)
                        sum_tokens(p.chunk)
                        scale_tokens(p.chunk, 0)
                    if p.out:
                        norm_out(p)
                    if p.attn:
                        scores(p)
                        softmax_shift(p)
                    elif p.out:
                        add_conv(p)
                    if p.ahead:
                        center_tokens(p.chunk + 1, 1 - p.parity, (p.t + 1) * CW)
                    if p.mlp:
                        add_mlp(p, 0)
                    if p.attn:
                        softmax_scale(p)
                    for d in range(3):
                        if p.attn:
                            values(p, d)
                        if p.mlp:
                            add_mlp(p, 1 + d)
                        if d == 0 and p.ahead:
                            sum_tokens(p.chunk + 1)
                    if p.mlp:
                        add_mlp(p, 4)
                        add_mlp(p, 5)
                    if p.ahead:
                        scale_tokens(p.chunk + 1, 1 - p.parity)
                    if p.first:
                        dve.wait_ge(xb_in, p.pair * (SETS * 16) + SETS * 16)
                        v.tensor_tensor(XB[:], XB[:], cbias[:].unsqueeze(2).broadcast_to([P, SETS * C, W]), ALU.add).then_inc(xb_ready, 1)
                        dve.wait_ge(xb_ready, p.pair + 1)
                    if p.attn:
                        for g in range(4):
                            add_attention(p, g)
                        norm_residual(p)

                steps(dve, body)

            @block.gpsimd
            def _(pool):
                g_ = nc.gpsimd

                def body(p):
                    if not p.attn:
                        return
                    k = p.chunk
                    pool.wait_ge(q_read, k * TW + TW + 2)
                    pool.wait_ge(c_read, p.c_base + 2)
                    for d in (-2, 2):
                        query_key(g_, d).then_inc(sc_p, 1)
                    for d in range(3):
                        y = PR[:, 3 * d, :]
                        for e in (1, 2):
                            pool.wait_ge(val_v, k * 9 + 3 * d + e + 1 + 9)
                            if e == 2:
                                pool.wait_ge(val_p, k * 6 + 2 * d + 1)
                            g_.tensor_tensor(y, y, PR[:, 3 * d + e, :], ALU.add).then_inc(val_p, 1)

                steps(pool, body)

            @block.scalar
            def _(act):
                s_ = nc.scalar
                act.sem_inc(t_read, 2)
                act.sem_inc(q_read, 2)
                act.sem_inc(f_read, 2)
                act.wait_ge(w_ready, 2)

                def inverse_std(var, r, sem_):
                    s_.activation(r, var, ACT.Abs_reciprocal_sqrt, bias=eps[:], scale=1.0 / EMB).then_inc(sem_, 1)

                def read_t(p, name, g, out, n):
                    k = p.t_at[name] + g
                    act.wait_ge(t_made, p.t_base + k + 1)
                    s_.activation(out, tps[0:F2, k % 2, 0:n * P].rearrange("f (w h) -> f w h", h=P), ACT.Copy).then_inc(t_read, 1)

                def gelu(p, g):
                    kb = p.behind
                    act.wait_ge(c_made, p.c_base + (p.c_at["mlp"] + g - 1 if g >= 2 else 0))
                    for m in range(3):
                        n = g * 3 + m
                        act.wait_ge(f_made, kb * 18 + n + 1)
                        s_.activation(G[:, g % 2, m, :], fps[:, n % 2, :], ACT.Gelu).then_inc(f_read, 1)

                def square_tokens(k, parity):
                    act.wait_ge(n1, k * 5 + 3)
                    s_.activation(hA[:], Tc[:, parity], ACT.Square).then_inc(n1_sq, 1)

                def std_tokens(k):
                    act.wait_ge(n1, k * 5 + 4)
                    inverse_std(st[:, 2, 0:TW * SETS], st[:, 3, 0:TW * SETS], n1_r)

                def read_qkv(k, ws):
                    for w in ws:
                        act.wait_ge(q_made, k * TW + w + 1)
                        s_.activation(QKV[:, w, :], qps[:, w % 2, 0:3 * F2], ACT.Copy).then_inc(q_read, 1)

                def read_tokens(p, name, g):
                    at, n = sum(T_WIDTHS[:g]), T_WIDTHS[g]
                    read_t(p, name, g, hAT[:, at:at + n, :], n)

                def square_residual(p, d):
                    act.wait_ge(c_read, p.c_base + p.c_at["proj"] + 2 * d + 2 + 2)
                    s_.activation(hB[:, d], x1c[:, d], ACT.Square).then_inc(n2_sq, 1)

                def square_out(p, d):
                    act.wait_ge(c_read, p.c_base + p.c_at["mlp"] + 6 + 2)
                    s_.activation(squares()[:, d * CW:(d + 1) * CW, :], x2c[:, d], ACT.Square).then_inc(n3_sq, 1)

                def body(p):
                    k = p.chunk
                    if p.first:
                        square_tokens(k, 0)
                        std_tokens(k)
                        for g in range(len(T_WIDTHS)):
                            read_tokens(p, "first", g)
                    if p.attn:
                        act.wait_ge(val_v, k * 9 + 9)
                        read_qkv(k, range(QKV_BEFORE_STD[0]))
                    if p.mlp:
                        act.wait_ge(n2, p.behind * 6 + 3)
                        inverse_std(st[:, 4, :], st[:, 5, :], n2_r)
                    if p.attn:
                        read_qkv(k, range(*QKV_BEFORE_STD))
                    if p.out:
                        act.wait_ge(n3, p.last * 4 + 1)
                        inverse_std(st[:, 6, :], st[:, 7, :], n3_r)
                    if p.attn:
                        read_qkv(k, range(QKV_BEFORE_STD[1], TW))
                    act.wait_ge(c_read, p.c_base + 2)
                    if p.mlp:
                        for g in range(6):
                            read_t(p, "norm2", g, hBT[:, g * 4:(g + 1) * 4, :], 4)
                    if p.out:
                        for g in range(2):
                            read_t(p, "norm3", g, zT[:, g * 4:(g + 1) * 4, :], 4)
                    if p.mlp:
                        for g in range(GELUS_BEFORE_EXP):
                            gelu(p, g)
                    if p.attn:
                        act.wait_ge(soft, k * 9 + 6)
                        s_.activation(At[:], At[:], ACT.Exp, scale=float(HEAD) ** -0.5).then_inc(soft_exp, 1)
                    if p.ahead:
                        square_tokens(k + 1, 1 - p.parity)
                    if p.mlp:
                        for g in range(GELUS_BEFORE_EXP, 6):
                            gelu(p, g)
                    if p.ahead:
                        std_tokens(k + 1)
                    if p.attn:
                        for g in range(6):
                            read_t(p, "mix", g, yT[:, g // 2, (g % 2) * 4:(g % 2) * 4 + 4, :], 4)
                    for g in range(3):
                        if p.mlp:
                            square_out(p, g)
                        if p.ahead:
                            read_tokens(p, "norm1", g)
                        if p.attn and g == 1:
                            square_residual(p, 0)
                    if p.ahead:
                        read_tokens(p, "norm1", 3)
                    if p.attn:
                        square_residual(p, 1)
                        square_residual(p, 2)

                steps(act, body)

def layer1(nc, x1, x2, pw, pair, w1):
    TILE = 1024
    NT = HW // TILE
    LOADS = 8
    with ExitStack() as ctx:
        def sb(name, shape, dt=F32):
            return ctx.enter_context(nc.sbuf_tensor(name, shape, dt))

        def sem(name):
            return ctx.enter_context(nc.semaphore(name))

        X = sb("l1_x", [P, HW])
        with ExitStack() as ctx1:
            def sb1(name, shape, dt=F32):
                return ctx1.enter_context(nc.sbuf_tensor(name, shape, dt))

            norm = Norm(nc, ctx1, "n1")
            G = sb1("l1_g", [P, HW])
            mats = sb1("l1_mats", [P, 5, P])
            vecs = sb1("l1_vecs", [P, 5])
            top = sb1("l1_top", [P, 8])
            stat = sb1("l1_stat", [P, 8])
            scaled = sb1("l1_scaled", [P, 2, P])
            fold = sb1("l1_fold", [P, 2, P])
            bias = sb1("l1_bias", [P, 2])
            gate = sb1("l1_gate", [P, 2, 2, TILE])
            mix = sb1("l1_mix", [P, 2, TILE])
            fps = ctx1.enter_context(nc.psum_tensor("l1_fps", [P, 2, 132], F32))
            gps = ctx1.enter_context(nc.psum_tensor("l1_gps", [P, 2, 2, 512], F32))
            ops = ctx1.enter_context(nc.psum_tensor("l1_ops", [P, 2, 512], F32))
            x_in = [sem(f"l1_x_in{k}") for k in range(LOADS)]
            w_in = sem("l1_w_in")
            chain = sem("l1_chain")
            top_chain = sem("l1_top_chain")
            g_ready = sem("l1_g_ready")
            scaled_ready = sem("l1_scaled_ready")
            fold_made = sem("l1_fold_made")
            fold_ready = sem("l1_fold_ready")
            pre_made = sem("l1_pre_made")
            tanh_done = sem("l1_tanh_done")
            gates_ready = sem("l1_gates_ready")
            sum_done = sem("l1_sum_done")
            mix_ready = sem("l1_mix_ready")
            out_made = sem("l1_out_made")
            out_done = sem("l1_out_done")
            stored = sem("l1_stored")
            with nc.Block() as block:
                @block.sync
                def _(sp):
                    for k in range(LOADS):
                        n = HW // LOADS
                        sp.dma_start(X[:, k * n:(k + 1) * n], x1[:, k * n:(k + 1) * n]).then_inc(x_in[k], 16)
                    norm.sync_part(sp, pair)
                    sp.dma_start(mats[:], w1[0]).then_inc(w_in, 16)
                    sp.dma_start(vecs[:], w1[1]).then_inc(w_in, 16)
                    for k in range(4):
                        n = HW // 4
                        sp.wait_ge(out_done, (k + 1) * NT // 4)
                        sp.dma_start(x2[:, k * n:(k + 1) * n], X[:, k * n:(k + 1) * n]).then_inc(stored, 16)
                    sp.wait_ge(stored, 4 * 16)

                @block.vector
                def _(dve):
                    v = nc.vector
                    link = Chain(dve, chain)
                    dve.sem_inc(mix_ready, 2)

                    def chunk_in(e, k):
                        if k % (norm.CHUNKS // LOADS) == 0:
                            e.wait_ge(x_in[k // (norm.CHUNKS // LOADS)], 16)

                    norm.vector_part(dve, link, lambda k, n: X[:, k * n:(k + 1) * n], chunk_in)
                    link(v.reduce_max(top[:, 0:1], X[:], AX.X))
                    link(v.tensor_scalar(stat[:, 0:1], norm.own[:, 0:1], norm.rstd[:], norm.shift[:], ALU.mult, ALU.add))
                    link(v.tensor_scalar(stat[:, 1:2], top[:, 0:1], norm.rstd[:], norm.shift[:], ALU.mult, ALU.add))
                    link(v.tensor_scalar(stat[:, 2:4], stat[:, 0:2], 1e-5, None, ALU.add))
                    link(v.reciprocal(stat[:, 4:6], stat[:, 2:4]))
                    dve.wait_ge(w_in, 32)
                    for m in range(2):
                        last = v.tensor_scalar(scaled[:, m, :], mats[:, 2 + m, :], stat[:, 4 + m:5 + m], None, ALU.mult)
                    last.then_inc(scaled_ready, 1)
                    dve.wait_ge(fold_made, 1)
                    v.tensor_copy(fold[:], fps[:, :, 0:P])
                    link(v.tensor_tensor(bias[:], fps[:, :, P], vecs[:, 2:4], ALU.add))
                    v.tensor_scalar(G[:], X[:], norm.rstd[:], norm.shift[:], ALU.mult, ALU.add).then_inc(g_ready, 1)
                    with dve.Fori(0, NT // 2) as it:
                        for j in range(2):
                            at = it * (2 * TILE) + j * TILE
                            dve.wait_ge(gates_ready, it * 2 + j + 1)
                            v.scalar_tensor_tensor(gate[:, j, 0, :], gate[:, j, 0, :], 1.0, gate[:, j, 1, :],
                                                   ALU.add, ALU.add).then_inc(sum_done, 1)
                            dve.wait_ge(sum_done, it * 2 + j + 1)
                            v.tensor_tensor(mix[:, j, :], gate[:, j, 0, :], G[:, bass.ds(at, TILE)],
                                            ALU.mult).then_inc(mix_ready, 1)
                            dve.wait_ge(out_made, it * 2 + j + 1)
                            xt = X[:, bass.ds(at, TILE)]
                            v.scalar_tensor_tensor(xt, ops[:].rearrange("p a n -> p (a n)"), vecs[:, 4:5], xt,
                                                   ALU.add, ALU.add).then_inc(out_done, 1)

                @block.tensor
                def _(pe):
                    t = nc.tensor
                    norm.tensor_part(pe)
                    pe.wait_ge(scaled_ready, 1)
                    for m in range(2):
                        t.matmul(fps[:, m, 0:P], mats[:, m, :], scaled[:, m, :], start=True, stop=True)
                        last = t.matmul(fps[:, m, P:P + 1], scaled[:, m, :], vecs[:, m:m + 1], start=True, stop=True)
                    last.then_inc(fold_made, 1)
                    pe.wait_ge(g_ready, 1)
                    with pe.Fori(0, NT // 2) as it:
                        for j in range(2):
                            at = it * (2 * TILE) + j * TILE
                            for m in range(2):
                                pe.wait_ge(tanh_done, it * 4 + j * 2 + m + 2)
                                for q in range(2):
                                    last = t.matmul(gps[:, m, q, :], fold[:, m, :], G[:, bass.ds(at + q * 512, 512)],
                                                    start=True, stop=True)
                                last.then_inc(pre_made, 1)
                            pe.wait_ge(mix_ready, it * 2 + j + 1 + 2)
                            for q in range(2):
                                last = t.matmul(ops[:, q, :], mats[:, 4, :], mix[:, j, q * 512:(q + 1) * 512],
                                                start=True, stop=True)
                            last.then_inc(out_made, 1)

                @block.scalar
                def _(act):
                    s = nc.scalar
                    act.sem_inc(tanh_done, 2)
                    norm.scalar_part(act)
                    act.wait_ge(g_ready, 1)
                    with act.Fori(0, NT // 2) as it:
                        for j in range(2):
                            act.wait_ge(mix_ready, it * 2 + j - 1 + 2)
                            for m in range(2):
                                act.wait_ge(pre_made, it * 4 + j * 2 + m + 1)
                                s.activation(gate[:, j, m, :], gps[:, m, :, :].rearrange("p a n -> p (a n)"),
                                             ACT.Tanh, bias=bias[:, m:m + 1]).then_inc(tanh_done, 1)
                            act.wait_ge(tanh_done, it * 4 + j * 2 + 2 + 2)
                            s.activation(gate[:, j, :, :], gate[:, j, :, :], ACT.Sigmoid).then_inc(gates_ready, 1)

        powers(nc, ctx, X, pw, pair)

def powers(nc, ctx, X, pw, pair):
    CH = SUB
    NCH = IMG // CH
    BUF = 3
    STORES = 3 * DEG
    with ExitStack() as ctx2:
        def sb(name, shape, dt=F32):
            return ctx2.enter_context(nc.sbuf_tensor(name, shape, dt))

        def sem(name):
            return ctx2.enter_context(nc.semaphore(name))

        norm = Norm(nc, ctx2, "n2")
        GP = sb("pw_g", [P, IMG])
        up = sb("pw_up", [P, DEG - 1, CH])
        hi = sb("pw_hi", [P, BUF, DEG, CH], BF16)
        mid = sb("pw_mid", [P, BUF, DEG, CH], BF16)
        lo = sb("pw_lo", [P, BUF, DEG, CH], BF16)
        rest = sb("pw_rest", [P, DEG, CH])
        chain = sem("pw_chain")
        zeroed = sem("pw_zeroed")
        padded = sem("pw_padded")
        up_ready = sem("pw_up_ready")
        hi_ready = sem("pw_hi_ready")
        rest_ready = sem("pw_rest_ready")
        mid_ready = sem("pw_mid_ready")
        lo_ready = sem("pw_lo_ready")
        stored = [sem(f"pw_stored{u}") for u in range(BUF)]
        with nc.Block() as block:
            @block.sync
            def _(sp):
                for u in range(BUF):
                    sp.sem_inc(stored[u], 16)
                norm.sync_part(sp, pair)
                lines = pw.rearrange("t c i (b n) -> t i b c n", b=NB)
                with sp.Fori(0, NCH // BUF) as it:
                    for u in range(BUF):
                        k = it * BUF + u
                        for part, (t, ready) in enumerate(((hi, hi_ready), (mid, mid_ready), (lo, lo_ready))):
                            sp.wait_ge(ready, k * DEG + DEG)
                            for i in range(DEG):
                                sp.dma_start(lines[part, i, :, :, bass.ds(k * CH, CH)], t[:, u, i, :]).then_inc(stored[u], 16)
                for u in range(BUF):
                    sp.wait_ge(stored[u], NCH // BUF * STORES * 16 + 16)

            @block.gpsimd
            def _(pool):
                nc.gpsimd.memset(GP[:], 0.0).then_inc(zeroed, 1)

            @block.vector
            def _(dve):
                v = nc.vector
                link = Chain(dve, chain)
                norm.vector_part(dve, link, lambda k, n: X[:, k * n:(k + 1) * n], lambda e, k: None)
                dve.wait_ge(zeroed, 1)
                v.tensor_scalar(image_rows(GP), X[:].rearrange("p (h w) -> p h w", w=W), norm.rstd[:], norm.shift[:],
                                ALU.mult, ALU.add).then_inc(padded, 1)
                dve.wait_ge(padded, 1)
                with dve.Fori(0, NCH // BUF) as it:
                  for u in range(BUF):
                    k = it * BUF + u
                    g = GP[:, bass.ds(k * CH, CH)]
                    of = [g] + [up[:, i, :] for i in range(DEG - 1)]
                    for i, (a, b) in enumerate(((0, 0), (1, 0), (1, 1), (3, 0))):
                        v.tensor_tensor(up[:, i, :], of[a], of[b], ALU.mult).then_inc(up_ready, 1)
                        dve.wait_ge(up_ready, k * (DEG - 1) + i + 1)
                    for i in range(DEG):
                        dve.wait_ge(hi_ready, k * DEG + i + 1)
                        v.tensor_tensor(rest[:, i, :], of[i], hi[:, u, i, :], ALU.subtract).then_inc(rest_ready, 1)
                    dve.wait_ge(stored[u], it * (STORES * 16) + 16)
                    for i in range(DEG):
                        dve.wait_ge(mid_ready, k * DEG + i + 1)
                        v.tensor_tensor(lo[:, u, i, :], rest[:, i, :], mid[:, u, i, :], ALU.subtract).then_inc(lo_ready, 1)
                    dve.wait_ge(lo_ready, k * DEG + DEG)

            @block.tensor
            def _(pe):
                norm.tensor_part(pe)

            @block.scalar
            def _(act):
                s = nc.scalar
                norm.scalar_part(act)
                act.wait_ge(padded, 1)
                with act.Fori(0, NCH // BUF) as it:
                  for u in range(BUF):
                    k = it * BUF + u
                    act.wait_ge(stored[u], it * (STORES * 16) + 16)
                    for i in range(DEG):
                        if i:
                            act.wait_ge(up_ready, k * (DEG - 1) + i)
                        src = up[:, i - 1, :] if i else GP[:, bass.ds(k * CH, CH)]
                        s.activation(hi[:, u, i, :], src, ACT.Copy).then_inc(hi_ready, 1)
                    for i in range(DEG):
                        act.wait_ge(rest_ready, k * DEG + i + 1)
                        s.activation(mid[:, u, i, :], rest[:, i, :], ACT.Copy).then_inc(mid_ready, 1)

NPP = len(AROUND) // 2
NPAIRED = NCG * NPP
NBLK = NPAIRED + 2
BODY = 6
SUBS = BODY * NSUB
STEPS = SUBS * NBLK
Q_BANKS, P_BANKS, A_RING, R_RING = 2, 3, 18, 9
assert NBLK % Q_BANKS == 0 and NBLK % P_BANKS == 0 and NBLK % A_RING == 0 and NBLK % R_RING == 0
ABS_DVE = {3, 7, 11, 15}
SQ_DVE = {4, 5, 12, 13}
LAG_ROOT, LAG_SQ, LAG_P, LAG_MUL, LAG_SUM, LAG_COPY = 3, 4, 7, 8, 10, 11
SHIFT_FROM, SHIFT_EVERY = 2 * NBLK - 10, 5
COPY_OUT = SHIFT_FROM + 7 * SHIFT_EVERY + 3
LOADED = SLOTS * NSUB * NBLK

def run_steps(engine, step):
    for s in range(LAG_COPY):
        step(0, s)
    with engine.Fori(0, NSUP // BODY) as it:
        for s in range(LAG_COPY, LAG_COPY + STEPS):
            step(it, s)

def among(members, s):
    return (s // NBLK) * len(members) + sum(n <= s % NBLK for n in members)

def layer2(nc, pw, l2w, out2):
    all_blocks = set(range(NBLK))
    abs_act = all_blocks - ABS_DVE
    sq_pool = all_blocks - SQ_DVE
    wcols = NPAIRED * P + NCG * P
    with ExitStack() as ctx:
        def sb(name, shape, dt=F32):
            return ctx.enter_context(nc.sbuf_tensor(name, shape, dt))

        def sem(name):
            return ctx.enter_context(nc.semaphore(name))

        wst = sb("l2_wst", [KROWS, 2, wcols], BF16)
        with ExitStack() as ctx0:
            raw = ctx0.enter_context(nc.sbuf_tensor("l2_raw", [KROWS, 2, wcols], F32))
            part = ctx0.enter_context(nc.sbuf_tensor("l2_part", [KROWS, wcols], BF16))
            total = ctx0.enter_context(nc.sbuf_tensor("l2_total", [KROWS, wcols], F32))
            mask = ctx0.enter_context(nc.sbuf_tensor("l2_mask", [KROWS, 3], F32))
            w_in = sem("l2_w_in")
            wchain = sem("l2_wchain")
            with nc.Block() as block:
                @block.sync
                def _(sp):
                    for k in range(2):
                        sp.dma_start(raw[:, k, :], l2w[k]).then_inc(w_in, 16)
                    sp.dma_start(mask[:], l2w[2]).then_inc(w_in, 16)

                @block.vector
                def _(dve):
                    v = nc.vector
                    link = Chain(dve, wchain)
                    dve.wait_ge(w_in, 48)
                    for k in range(2):
                        link(v.tensor_copy(part[:], raw[:, k, :]))
                        link(v.tensor_scalar(total[:], part[:], mask[:, 0:1], None, ALU.mult))
                        for m in (1, 2):
                            link(v.tensor_tensor(raw[:, k, :], raw[:, k, :], part[:], ALU.subtract))
                            link(v.tensor_copy(part[:], raw[:, k, :]))
                            link(v.scalar_tensor_tensor(total[:], part[:], mask[:, m:m + 1], total[:], ALU.mult, ALU.add))
                        link(v.tensor_copy(wst[:, k, :], total[:]))

        sums = sb("l2_sums", [P, 2, 32])
        pick = sb("l2_pick", [P, len(AROUND), 32])
        mv = sb("l2_mv", [KROWS, SLOTS, NCG, SUP], BF16)
        A = sb("l2_a", [P, A_RING, SUB])
        R = sb("l2_r", [P, R_RING, SUB])
        S = sb("l2_s", [P, SLOTS, SUP])
        O = sb("l2_o", [P, 2, SUB])
        qps = ctx.enter_context(nc.psum_tensor("l2_qps", [P, Q_BANKS, 512], F32))
        pps = ctx.enter_context(nc.psum_tensor("l2_pps", [P, P_BANKS, 512], F32))
        sps = ctx.enter_context(nc.psum_tensor("l2_sps", [P, 512], F32))
        ops = ctx.enter_context(nc.psum_tensor("l2_ops", [P, 2, 512], F32))
        c_in = sem("l2_c_in")
        mv_in = [sem(f"l2_mv_in{k}") for k in range(SLOTS)]
        cleared = sem("l2_cleared")
        q_made = sem("l2_q_made")
        p_made = sem("l2_p_made")
        abs_a, abs_v = sem("l2_abs_a"), sem("l2_abs_v")
        root_done = sem("l2_root_done")
        sq_v, sq_p = sem("l2_sq_v"), sem("l2_sq_p")
        mul_done = sem("l2_mul_done")
        summed = sem("l2_summed")
        s_copied = sem("l2_s_copied")
        o_made = sem("l2_o_made")
        o_copied = sem("l2_o_copied")
        stored = [sem("l2_stored0"), sem("l2_stored1")]

        def wait_abs(e, it, s):
            if s % NBLK in ABS_DVE:
                e.wait_ge(abs_v, it * (SUBS * len(ABS_DVE)) + among(ABS_DVE, s))
            else:
                e.wait_ge(abs_a, it * (SUBS * len(abs_act)) + among(abs_act, s))

        def wait_square(e, it, s):
            s |= 1
            for members, done in ((SQ_DVE, sq_v), (sq_pool, sq_p)):
                if s % NBLK in members:
                    e.wait_ge(done, it * (SUBS * len(members)) + among(members, s))

        with nc.Block() as block:
            @block.sync
            def _(sp):
                sp.dma_start(sums[:], l2w[3]).then_inc(c_in, 16)
                sp.dma_start(pick[:], l2w[4]).then_inc(c_in, 16)
                sp.sem_inc(stored[0], 16)
                sp.sem_inc(stored[1], 16)
                sp.wait_ge(cleared, 3)

                def load(g, u, made):
                    sp.wait_ge(p_made, made)
                    rows = 0
                    for x_part, times in ((0, 3), (1, 2), (2, 1)):
                        for r in range(times):
                            for cg in range(NCG):
                                src = pw[x_part, cg * CG:(cg + 1) * CG, :, bass.ds(g * SUP, SUP)].rearrange("c i n -> (c i) n")
                                sp.dma_start(mv[rows:rows + CG * DEG, u, cg, :], src).then_inc(mv_in[u], 16)
                            rows += CG * DEG

                def load_supertile(g, u):
                    load(g, u % SLOTS, (g + 1) * (NBLK * NSUB))

                def store(n, bank):
                    sp.wait_ge(o_copied, n + 1 + 1)
                    for j in range(NSUB):
                        sp.dma_start(out2[:, bass.ds(n * SUP + j * SUB, SUB)], O[32 * j:32 * j + C, bank, :]).then_inc(stored[bank], 16)

                for g in range(SLOTS):
                    load_supertile(g, g)
                with sp.Fori(0, NSUP // BODY - 1) as it:
                    for u in range(BODY):
                        load_supertile(it * BODY + u + SLOTS, u)
                        store(it * BODY + u, (u + 1) % 2)
                for g in range(NSUP - BODY, NSUP + 1):
                    if g + SLOTS < NSUP:
                        load_supertile(g + SLOTS, g)
                    elif g + SLOTS == NSUP:
                        load(0, 0, (NSUP + 1) * NBLK * NSUB)
                    store(g, (g + 1) % 2)
                sp.wait_ge(stored[0], NSUP // 2 * NSUB * 16 + 16)
                sp.wait_ge(stored[1], (NSUP // 2 + 1) * NSUB * 16 + 16)

            @block.gpsimd
            def _(pool):
                g = nc.gpsimd
                g.memset(mv[:], 1.0).then_inc(cleared, 1)
                g.memset(S[:], 0.0).then_inc(cleared, 1)
                g.memset(O[:], 0.0).then_inc(cleared, 1)
                pool.wait_ge(cleared, 3)

                def step(it, s):
                    m = s - LAG_SQ
                    if m >= 0 and m % 2 == 0 and m % NBLK in sq_pool:
                        a = A[:, m % A_RING:m % A_RING + 2, :]
                        pool.wait_ge(root_done, it * STEPS + m + 2)
                        g.tensor_tensor(a, a, a, ALU.mult).then_inc(sq_p, 2)

                run_steps(pool, step)

            @block.tensor
            def _(pe):
                t = nc.tensor

                def product(k, s, out):
                    sub, n = divmod(s, NBLK)
                    cols = slice((sub % NSUB) * SUB, (sub % NSUB + 1) * SUB)
                    x = mv[:, (sub // NSUB) % SLOTS]
                    if n < NPAIRED:
                        return t.matmul(out, wst[:, k, n * P:(n + 1) * P], x[:, n // NPP, cols], start=True, stop=True)
                    for cg in (2 * (n - NPAIRED), 2 * (n - NPAIRED) + 1):
                        at = NPAIRED * P + cg * P
                        last = t.matmul(out, wst[:, k, at:at + P], x[:, cg, cols],
                                        start=cg % 2 == 0, stop=cg % 2 == 1)
                    return last

                def shifted_sum(k, bank, slot):
                    for j in range(NSUB):
                        a = 0
                        while a < SUB:
                            src = j * SUB + OFFS[AROUND[k]] + a
                            where, src = src // SUP, src % SUP
                            n = min(SUB - a, SUP - src)
                            last = t.matmul(ops[32 * j:32 * j + 32, bank, a:a + n], pick[:, k, :],
                                            S[:, (slot + where) % SLOTS, src:src + n],
                                            start=False, stop=k == len(AROUND) - 1, skip_group_check=True)
                            a += n
                    if k == len(AROUND) - 1:
                        last.then_inc(o_made, 1)

                pe.sem_inc(p_made, LOADED)
                pe.sem_inc(summed, R_RING)
                pe.wait_ge(c_in, 32)
                pe.wait_ge(cleared, 3)
                for j in range(NSUB):
                    t.matmul(ops[32 * j:32 * j + 32, 1, 0:SUB], sums[:, 0, :], S[:, 2, 0:SUB], start=True, stop=False,
                             skip_group_check=True)

                def step(it, s):
                    sub, n = divmod(s, NBLK)
                    if n == 0 and sub % NSUB == 0:
                        u = sub // NSUB
                        pe.wait_ge(mv_in[u % SLOTS], (it * (BODY // SLOTS) + u // SLOTS + 1) * (6 * NCG * 16))
                    if s >= Q_BANKS:
                        wait_abs(pe, it, s - Q_BANKS)
                    product(1, s, qps[:, s % Q_BANKS, 0:SUB]).then_inc(q_made, 1)
                    m = s - LAG_P
                    if m >= 0:
                        pe.wait_ge(mul_done, it * STEPS + m - P_BANKS + 1 + A_RING)
                        product(0, m, pps[:, m % P_BANKS, 0:SUB]).then_inc(p_made, 1)
                    m = s - LAG_SUM
                    if m < 0:
                        return
                    sub, n = divmod(m, NBLK)
                    u, j = divmod(sub, NSUB)
                    if n < NPAIRED and n % NPP == NPP - 1:
                        pe.wait_ge(mul_done, it * STEPS + m + 1 + A_RING)
                        if n == NPP - 1:
                            pe.wait_ge(s_copied, it * SUBS + sub + 1)
                        for pp in range(NPP):
                            last = t.matmul(sps[32 * pp:32 * pp + 32, 0:SUB], sums[:, 0, :],
                                            R[:, (m - NPP + 1 + pp) % R_RING, :], start=n == NPP - 1,
                                            stop=n == NPAIRED - 1, skip_group_check=True)
                        last.then_inc(summed, NPP)
                    if n >= NPAIRED:
                        pe.wait_ge(mul_done, it * STEPS + m + 1 + A_RING)
                        if n == NPAIRED and j == 0:
                            pe.wait_ge(o_copied, it * BODY + u + 1)
                        t.matmul(ops[32 * j:32 * j + 32, u % 2, 0:SUB], sums[:, 1, :], R[:, m % R_RING, :],
                                 start=n == NPAIRED, stop=False, skip_group_check=True).then_inc(summed, 1)
                    k, odd = divmod(m % (NBLK * NSUB) - SHIFT_FROM, SHIFT_EVERY)
                    if 0 <= k < len(AROUND) and not odd:
                        if k == 0:
                            pe.wait_ge(s_copied, it * SUBS + u * NSUB + 1 + 1)
                        shifted_sum(k, (u + 1) % 2, (u - 1) % SLOTS)

                run_steps(pe, step)
                pe.wait_ge(s_copied, NSUP * NSUB + 1)
                for k in range(len(AROUND)):
                    shifted_sum(k, 1, (BODY - 1) % SLOTS)

            @block.vector
            def _(dve):
                v = nc.vector
                dve.sem_inc(mul_done, A_RING)

                def step(it, s):
                    if s % NBLK in ABS_DVE:
                        dve.wait_ge(q_made, it * STEPS + s + 1)
                        dve.wait_ge(mul_done, it * STEPS + s + 1)
                        v.tensor_scalar(A[:, s % A_RING, :].bitcast(I32), qps[:, s % Q_BANKS, 0:SUB].bitcast(I32),
                                        0x7FFFFFFF, None, ALU.bitwise_and).then_inc(abs_v, 1)
                    m = s - LAG_SQ
                    if m >= 0 and m % 2 == 0 and m % NBLK in SQ_DVE:
                        a = A[:, m % A_RING:m % A_RING + 2, :]
                        dve.wait_ge(root_done, it * STEPS + m + 2)
                        v.tensor_tensor(a, a, a, ALU.mult).then_inc(sq_v, 2)
                    m = s - LAG_MUL
                    if m >= 0:
                        wait_square(dve, it, m)
                        dve.wait_ge(p_made, it * STEPS + m + 1 + LOADED)
                        dve.wait_ge(summed, it * STEPS + m + 1)
                        v.tensor_tensor(R[:, m % R_RING, :], pps[:, m % P_BANKS, 0:SUB], A[:, m % A_RING, :],
                                        ALU.mult).then_inc(mul_done, 1)

                run_steps(dve, step)

            @block.scalar
            def _(act):
                s_ = nc.scalar

                act.sem_inc(s_copied, 1)
                act.sem_inc(o_copied, 1)

                def copy_out(bank, n, done):
                    act.wait_ge(o_made, n + 1)
                    act.wait_ge(stored[bank], done + 16)
                    s_.activation(O[:, bank, :], ops[:, bank, 0:SUB], ACT.Copy).then_inc(o_copied, 1)

                act.wait_ge(cleared, 3)

                def step(it, s):
                    if s % NBLK in abs_act:
                        act.wait_ge(q_made, it * STEPS + s + 1)
                        act.wait_ge(mul_done, it * STEPS + s + 1)
                        s_.activation(A[:, s % A_RING, :], qps[:, s % Q_BANKS, 0:SUB], ACT.Abs).then_inc(abs_a, 1)
                    m = s - LAG_ROOT
                    if m >= 0 and m % 2 == 0:
                        a = A[:, m % A_RING:m % A_RING + 2, :]
                        wait_abs(act, it, m)
                        wait_abs(act, it, m + 1)
                        s_.activation(a, a, ACT.Abs_reciprocal_sqrt, bias=1.0).then_inc(root_done, 2)
                    m = s - LAG_COPY
                    if m < 0:
                        return
                    sub, n = divmod(m, NBLK)
                    u, j = divmod(sub, NSUB)
                    if n == NPAIRED - 1:
                        act.wait_ge(summed, it * STEPS + m + 1 + R_RING)
                        s_.activation(S[:, u % SLOTS, j * SUB:(j + 1) * SUB], sps[:, 0:SUB], ACT.Copy).then_inc(s_copied, 1)
                    if m % (NBLK * NSUB) == COPY_OUT:
                        copy_out((u + 1) % 2, it * BODY + u, (it * (BODY // 2) + u // 2) * (NSUB * 16))

                run_steps(act, step)
                copy_out(1, NSUP, NSUP // 2 * NSUB * 16)

SPLINE = 8
GRID_STEP = 2.0 / 5

def layer3(nc, x2, out2, pair, l3w, x3q, g3q, s3q, oq, out):
    with ExitStack() as ctx:
        def sem(name):
            return ctx.enter_context(nc.semaphore(name))

        with ExitStack() as ctx1:
            def sb1(name, shape, dt=F32):
                return ctx1.enter_context(nc.sbuf_tensor(name, shape, dt))

            norm = Norm(nc, ctx1, "n3")
            X = sb1("l3_x", [P, HW])
            Y = sb1("l3_y", [P, IMG])
            XP = sb1("l3_xp", [P, IMG])
            zero = sb1("l3_zero", [C, MARGIN + SUP])
            x_in, y_in = sem("l3_x_in"), sem("l3_y_in")
            chain = sem("l3_chain")
            x_ready, g_ready, s_ready, zeroed = sem("l3_x_ready"), sem("l3_g_ready"), sem("l3_s_ready"), sem("l3_zeroed")
            x_stored, stored = sem("l3_x_stored"), sem("l3_stored")

            with nc.Block() as block:
                @block.sync
                def _(sp):
                    norm.sync_part(sp, pair)
                    sp.dma_start(X[:], x2).then_inc(x_in, 16)
                    for b in range(NB):
                        sp.dma_start(Y[b * C:(b + 1) * C, :], out2[:, SUP + b * IMG:SUP + (b + 1) * IMG]).then_inc(y_in, 16)
                    sp.wait_ge(x_ready, 1)
                    for b in range(NB):
                        sp.dma_start(x3q[:, SUP + b * IMG:SUP + (b + 1) * IMG], XP[b * C:(b + 1) * C, :]).then_inc(x_stored, 16)
                    sp.wait_ge(g_ready, 1)
                    for b in range(NB):
                        sp.dma_start(g3q[:, b * IMG:(b + 1) * IMG], Y[b * C:(b + 1) * C, :]).then_inc(stored, 16)
                    sp.wait_ge(s_ready, 1)
                    for b in range(NB):
                        sp.dma_start(s3q[:, MARGIN + SUP + b * IMG:MARGIN + SUP + (b + 1) * IMG], XP[b * C:(b + 1) * C, :]).then_inc(stored, 16)
                    sp.wait_ge(zeroed, 1)
                    sp.dma_start(x3q[:, 0:SUP], zero[:, 0:SUP]).then_inc(stored, 16)
                    sp.dma_start(s3q[:, 0:MARGIN + SUP], zero[:]).then_inc(stored, 16)
                    sp.dma_start(s3q[:, MARGIN + SUP + LINE:], zero[:, 0:MARGIN]).then_inc(stored, 16)
                    sp.wait_ge(x_stored, NB * 16)
                    sp.wait_ge(stored, (2 * NB + 3) * 16)

                @block.gpsimd
                def _(pool):
                    g = nc.gpsimd
                    g.memset(zero[:], 0.0).then_inc(zeroed, 1)
                    pool.wait_ge(x_ready, 1)
                    g.memset(Y[:, 0:PW], 0.0).then_inc(zeroed, 1)
                    g.memset(Y[:, PW:PW + H * PW].rearrange("p (h w) -> p h w", w=PW)[:, :, 0:1], 0.0).then_inc(zeroed, 1)
                    g.memset(Y[:, PW + H * PW:], 0.0).then_inc(zeroed, 1)

                @block.vector
                def _(dve):
                    v = nc.vector
                    link = Chain(dve, chain)
                    link(v.memset(XP[:], 0.0))
                    dve.wait_ge(x_in, 16)
                    dve.wait_ge(y_in, NB * 16)
                    link(v.tensor_tensor(X[:], X[:], image_rows(Y), ALU.add))
                    v.tensor_copy(image_rows(XP), X[:].rearrange("p (h w) -> p h w", w=W)).then_inc(x_ready, 1)
                    norm.vector_part(dve, link, lambda k, n: X[:, k * n:(k + 1) * n], lambda e, k: None)
                    dve.wait_ge(zeroed, 4)
                    v.tensor_scalar(image_rows(Y), X[:].rearrange("p (h w) -> p h w", w=W), norm.rstd[:], norm.shift[:],
                                    ALU.mult, ALU.add).then_inc(g_ready, 1)

                @block.tensor
                def _(pe):
                    norm.tensor_part(pe)

                @block.scalar
                def _(act):
                    norm.scalar_part(act)
                    act.wait_ge(g_ready, 1)
                    act.wait_ge(x_stored, NB * 16)
                    nc.scalar.activation(XP[:], Y[:], ACT.Silu).then_inc(s_ready, 1)

        def sb(name, shape, dt=F32):
            return ctx.enter_context(nc.sbuf_tensor(name, shape, dt))

        sw = sb("l3_sw", [P, 9, 9, C])
        scaler = sb("l3_scaler", [P, 9, 9, C])
        bw = sb("l3_bw", [P, 2, 9, C])
        wsp = sb("l3_wsp", [P, 9, 32])
        wba = sb("l3_wba", [P, 2, 32])
        place = sb("l3_place", [P, 1])
        ends = sb("l3_ends", [P, 2])
        cbias = sb("l3_cbias", [P, 1])
        gx = sb("l3_gx", [P, 2, SUP])
        a = sb("l3_a", [P, SUP])
        b = sb("l3_b", [P, SUP])
        a2 = sb("l3_a2", [P, SUP])
        b2 = sb("l3_b2", [P, SUP])
        B = sb("l3_bases", [P, BODY, SUP])
        si = sb("l3_si", [P, 2, SUP])
        si0 = sb("l3_si0", [P, 2, SUP])
        xr = sb("l3_xr", [P, 2, SUB])
        O = sb("l3_o", [P, 2, SUB])
        ops = ctx.enter_context(nc.psum_tensor("l3_ops", [P, 2, 512], F32))
        w_in = sem("l3_w_in")
        wchain = sem("l3_wchain")
        w_ready, cleared = sem("l3_w_ready"), sem("l3_cleared")
        gx_in = [sem("l3_gx_in0"), sem("l3_gx_in1")]
        si_in = [sem("l3_si_in0"), sem("l3_si_in1")]
        v_done, a_done, a2_done, b2_done = (sem(f"l3_{n}_done") for n in ("v", "a", "a2", "b2"))
        b_done = sem("l3_b_done")
        cube_a, cube_b, bases = sem("l3_cube_a"), sem("l3_cube_b"), sem("l3_bases_ready")
        o_made = sem("l3_o_made")
        o_done = sem("l3_o_done")
        out_stored = sem("l3_out_stored")
        stored = [sem("l3_o_stored0"), sem("l3_o_stored1")]
        STORE = NSUB * 16
        with nc.Block() as block:
            @block.sync
            def _(sp):
                for t, src in ((sw, l3w[0]), (scaler, l3w[1]), (bw, l3w[2]), (place, l3w[3]), (cbias, l3w[4])):
                    sp.dma_start(t[:], src).then_inc(w_in, 16)
                sp.sem_inc(stored[0], 16)
                sp.sem_inc(stored[1], 16)
                sp.wait_ge(cleared, 7)

                def load_bases_input(g, k, used):
                    sp.wait_ge(b_done, used)
                    src = g3q[:, bass.ds(g * SUP, SUP)].unsqueeze(0).broadcast_to([SPLINE, C, SUP])
                    sp.dma_start(gx[:, k, :], src).then_inc(gx_in[k], 16)

                def load_silu(g, k):
                    sp.wait_ge(o_done, g + 1)
                    for r, p in enumerate(AROUND):
                        sp.dma_start(si[r * C:(r + 1) * C, k, :], s3q[:, bass.ds(g * SUP + (MARGIN + OFFS[p]), SUP)]).then_inc(si_in[k], 16)
                    sp.dma_start(si0[0:C, k, :], s3q[:, bass.ds(g * SUP + MARGIN, SUP)]).then_inc(si_in[k], 16)
                    for j in range(NSUB):
                        sp.dma_start(xr[32 * j:32 * j + C, k, :], x3q[:, bass.ds(g * SUP + j * SUB, SUB)]).then_inc(si_in[k], 16)

                def store(g, k):
                    sp.wait_ge(o_done, g + 3)
                    for j in range(NSUB):
                        sp.dma_start(oq[:, bass.ds(g * SUP + j * SUB, SUB)], O[32 * j:32 * j + C, k, :]).then_inc(stored[k], 16)

                load_bases_input(0, 0, 1)
                for g in (0, 1):
                    load_bases_input(g + 1, (g + 1) % 2, g + 2)
                    load_silu(g, g)
                with sp.Fori(1, NSUP // 2 - 1) as it:
                    for k in range(2):
                        g = it * 2 + k
                        load_bases_input(g + 1, 1 - k, g + 2)
                        load_silu(g, k)
                        store(g - 2, k)
                load_bases_input(NSUP - 1, 1, NSUP)
                for g in (NSUP - 2, NSUP - 1, NSUP):
                    load_silu(g, g % 2)
                    store(g - 2, g % 2)
                store(NSUP - 1, 1)
                store(NSUP, 0)
                sp.wait_ge(stored[0], (NSUP // 2 + 1) * STORE + 16)
                sp.wait_ge(stored[1], NSUP // 2 * STORE + 16)
                for n in range(NB):
                    src = oq[:, SUP + n * IMG + PW:SUP + n * IMG + PW + H * PW].rearrange("c (h w) -> c h w", w=PW)[:, :, 1:1 + W]
                    sp.dma_start(out[n], src).then_inc(out_stored, 16)
                sp.wait_ge(out_stored, NB * 16)

            @block.gpsimd
            def _(pool):
                g_ = nc.gpsimd
                for t, value in ((si0, 0.0), (xr, 0.0), (B, 0.0), (wsp, 0.0), (wba, 0.0)):
                    g_.memset(t[:], value).then_inc(cleared, 1)
                g_.memset(ends[:, 0:1], 2.0).then_inc(cleared, 1)
                g_.memset(ends[:, 1:2], 1.0).then_inc(cleared, 1)

            @block.scalar
            def _(act):
                s_ = nc.scalar
                act.sem_inc(b_done, 2)
                act.wait_ge(w_in, 80)
                act.wait_ge(cleared, 7)
                with act.Fori(0, NSUP // BODY) as it:
                    for u in range(BODY):
                        g = it * BODY + u
                        x = gx[:, u % 2, :]
                        act.wait_ge(gx_in[u % 2], (it * (BODY // 2) + u // 2 + 1) * 16)
                        s_.activation(x, x, ACT.Abs, bias=place[:], scale=1.0 / GRID_STEP).then_inc(v_done, 1)
                        act.wait_ge(v_done, g + 1)
                        act.wait_ge(cube_a, g + 1)
                        s_.activation(a[:], x, ACT.Relu, bias=ends[:, 0:1], scale=-1.0).then_inc(a_done, 1)
                        act.wait_ge(cube_b, g + 1)
                        s_.activation(b[:], x, ACT.Relu, bias=ends[:, 1:2], scale=-1.0).then_inc(b_done, 1)
                        act.wait_ge(a_done, g + 1)
                        act.wait_ge(bases, g + 1)
                        s_.activation(a2[:], a[:], ACT.Square).then_inc(a2_done, 1)
                        act.wait_ge(b_done, g + 1 + 2)
                        s_.activation(b2[:], b[:], ACT.Square).then_inc(b2_done, 1)

            @block.vector
            def _(dve):
                v = nc.vector
                link = Chain(dve, wchain)
                dve.sem_inc(o_done, 2)
                for used in (cube_a, cube_b, bases):
                    dve.sem_inc(used, 1)
                dve.wait_ge(w_in, 80)
                dve.wait_ge(cleared, 7)
                link(v.tensor_tensor(sw[:], sw[:], scaler[:], ALU.mult))
                link(v.tensor_reduce(scaler[:, 0, :, :], sw[:].rearrange("p m n f -> p n f m"), AX.X, ALU.add))
                link(v.tensor_scalar(wsp[:, :, 0:C], scaler[:, 0, :, :], 1.0 / 6, None, ALU.mult))
                v.tensor_reduce(wba[:, :, 0:C], bw[:].rearrange("p k m f -> p k f m"), AX.X, ALU.add).then_inc(w_ready, 1)

                def finish(g, k, before):
                    dve.wait_ge(o_made, g + 1 + 4)
                    dve.wait_ge(stored[k], before * STORE + 16)
                    v.scalar_tensor_tensor(O[:, k, :], ops[:, k, 0:SUB], cbias[:], xr[:, k, :],
                                           ALU.add, ALU.add).then_inc(o_done, 1)

                with dve.Fori(0, NSUP // BODY) as it:
                    for u in range(BODY):
                        g = it * BODY + u
                        dve.wait_ge(a2_done, g + 1)
                        v.tensor_tensor(a2[:], a2[:], a[:], ALU.mult).then_inc(cube_a, 1)
                        dve.wait_ge(b2_done, g + 1)
                        v.scalar_tensor_tensor(b2[:], b2[:], -4.0, b[:], ALU.mult, ALU.mult).then_inc(cube_b, 1)
                        dve.wait_ge(cube_b, g + 1 + 1)
                        dve.wait_ge(o_made, g + 1)
                        v.tensor_tensor(B[:, u, :], a2[:], b2[:], ALU.add).then_inc(bases, 1)
                        if u:
                            finish(g - 1, (u - 1) % 2, it * (BODY // 2) + (u - 1) // 2)
                    finish(it * BODY + BODY - 1, (BODY - 1) % 2, it * (BODY // 2) + (BODY - 1) // 2)
                finish(NSUP, 0, NSUP // 2)

            @block.tensor
            def _(pe):
                t = nc.tensor
                pe.sem_inc(o_made, 4)
                pe.wait_ge(w_ready, 1)

                def convolve(slot, k):
                    bank = ops[:, k, :]
                    for n, (w, x) in enumerate(((wba[:, 0, :], si), (wba[:, 1, :], si0))):
                        for j in range(NSUB):
                            t.matmul(bank[32 * j:32 * j + 32, 0:SUB], w, x[:, k, j * SUB:(j + 1) * SUB],
                                     start=n == 0, stop=False, skip_group_check=True)
                    for p in range(9):
                        for j in range(NSUB):
                            at = 0
                            while at < SUB:
                                src = j * SUB + OFFS[p] + at
                                where, src = src // SUP, src % SUP
                                n = min(SUB - at, SUP - src)
                                last = t.matmul(bank[32 * j:32 * j + 32, at:at + n], wsp[:, p, :],
                                                B[:, (slot + where) % BODY, src:src + n],
                                                start=False, stop=p == 8, skip_group_check=True)
                                at += n
                    last.then_inc(o_made, 1)

                with pe.Fori(0, NSUP // BODY) as it:
                    for u in range(BODY):
                        g = it * BODY + u
                        pe.wait_ge(bases, g + 1 + 1)
                        pe.wait_ge(si_in[u % 2], (it * (BODY // 2) + u // 2 + 1) * (13 * 16))
                        pe.wait_ge(o_done, g + 1)
                        convolve((u - 1) % BODY, u % 2)
                pe.wait_ge(si_in[0], (NSUP // 2 + 1) * (13 * 16))
                pe.wait_ge(o_done, NSUP + 1)
                convolve(BODY - 1, 0)

def build(nc, io, stages=(0, 1, 2, 3)):
    nc.disable_value_cache = True

    def dram(name, shape, dt=F32):
        return nc.dram_tensor(name, shape, dt, kind="Internal").ap()

    x1 = dram("x1", (P, HW))
    x2 = dram("x2", (P, HW))
    pw = dram("pw", (3, C, DEG, LINE), BF16)
    out2 = dram("out2", (C, SUP + LINE))
    x3q = dram("x3q", (C, SUP + LINE))
    g3q = dram("g3q", (C, LINE))
    s3q = dram("s3q", (C, MARGIN + SUP + LINE + MARGIN))
    oq = dram("oq", (C, SUP + LINE))
    x = io["x"].rearrange("b c h w -> (b c) (h w)")
    if 0 in stages:
        g0 = dram("g0", (P, H, W + 2))
        norm0(nc, x, io["pair"], g0)
        layer0(nc, io, g0, x1)
    if 1 in stages:
        layer1(nc, x1 if 0 in stages else x, x2, pw, io["pair"], (io["w1_mats"], io["w1_vecs"]))
    if 2 in stages:
        layer2(nc, pw, (io["w2_p"], io["w2_q"], io["w2_mask"], io["w2_sums"], io["w2_pick"]), out2)
    if 3 in stages:
        layer3(nc, x2, out2, io["pair"],
               (io["w3_spline"], io["w3_scaler"], io["w3_base"], io["w3_place"], io["w3_bias"]),
               x3q, g3q, s3q, oq, io["out"])

def lay_out(inputs):
    import numpy as np

    def diagonal(m, times):
        rows, cols = m.shape
        full = np.zeros((times * rows, times * cols), m.dtype)
        for k in range(times):
            full[k * rows:(k + 1) * rows, k * cols:(k + 1) * cols] = m
        return full

    a = {k: np.ascontiguousarray(v) for k, v in inputs.items()}
    f32 = np.float32
    got = {"x": a["x"]}
    got["pair"] = diagonal(np.full((2, 2), 0.5, f32), P // 2)
    wa = a["L0_conv_w_attn"]
    order = np.array([c * 3 + i for i in range(3) for c in range(C)])
    qkv = np.zeros((2, 48, 3, 2, 48), f32)
    for s in range(2):
        for k in range(3):
            qkv[s, :, k, s, :] = wa[k * 48:(k + 1) * 48][:, order].T
    got["w0_qkv"] = qkv.reshape(96, 288)
    got["w0_proj"] = diagonal(a["L0_conv_w_attn_proj"][order], 2)
    fc = np.zeros((2, 48, 2, 192), f32)
    for s in range(2):
        fc[s, :, s, :] = a["L0_conv_w_fc"][:, order].T
    got["w0_fc"] = fc.reshape(96, 384)
    got["w0_fc_proj"] = diagonal(a["L0_conv_w_fc_proj"][order], 2)
    got["w0_conv"] = diagonal(a["L0_conv_conv_w"][:, order].T, 2)
    got["w0_bias"] = np.ascontiguousarray(np.broadcast_to(np.tile(a["L0_conv_conv_b"], 2), (P, 2 * C)))
    got["ident"] = np.eye(P, dtype=f32)
    got["w0_center"] = diagonal((np.eye(48) - 1.0 / 48).astype(f32), 2)
    got["w1_mats"] = np.ascontiguousarray(np.stack(
        [diagonal(a["L1_conv_" + n], NB) for n in ("Wc", "W1")]
        + [diagonal(a["L1_conv_" + n].T, NB) for n in ("W2", "W3", "W4")], axis=1))
    got["w1_vecs"] = np.ascontiguousarray(np.stack([np.tile(a["L1_conv_" + n], NB) for n in ("bc", "b1", "b2", "b3", "b4")], axis=1))
    for name, src in (("w2_p", a["L2_conv_A"]), ("w2_q", a["L2_conv_Bc"])):
        full = np.zeros((C, C, 9, DEG + 1), f32)
        full[..., :DEG + 1 if name == "w2_p" else 0] = src if name == "w2_p" else 0
        if name == "w2_q":
            full[..., 1:1 + src.shape[-1]] = src
        paired = np.zeros((KROWS, NCG, NPP, CG, 2, C), f32)
        centre = np.zeros((KROWS, NCG, 8, C), f32)
        for cg in range(NCG):
            for c in range(CG):
                w = full[:, cg * CG + c]
                for j in range(len(X_PARTS)):
                    rows = slice(j * CG * DEG + c * DEG, j * CG * DEG + (c + 1) * DEG)
                    for k, p in enumerate(AROUND):
                        paired[rows, cg, k // 2, c, k % 2, :] = w[:, p, 1:].T
                    centre[rows, cg, (cg % 2) * CG + c, :] = w[:, CENTER, 1:].T
                for k, p in enumerate(AROUND):
                    paired[-3:, cg, k // 2, c, k % 2, :] = w[:, p, 0]
                centre[-3:, cg, (cg % 2) * CG + c, :] = w[:, CENTER, 0]
        got[name] = np.ascontiguousarray(np.concatenate([paired.reshape(KROWS, -1), centre.reshape(KROWS, -1)], axis=1))
    mask = np.zeros((KROWS, 3), f32)
    for j, part in enumerate(A_PARTS):
        mask[j * CG * DEG:(j + 1) * CG * DEG, part] = 1
    mask[-3:] = np.eye(3)
    got["w2_mask"] = mask
    sums = np.zeros((P, 2, 32), f32)
    sums[np.arange(P), 0, np.arange(P) % 32] = 1
    sums[np.arange(P), 1, np.arange(P) % C] = 1
    got["w2_sums"] = sums
    pick = np.zeros((P, len(AROUND), 32), f32)
    pick[np.arange(P), np.arange(P) // C, np.arange(P) % C] = 1
    got["w2_pick"] = pick
    sw = a["L3_conv_spline_weight"].transpose(4, 1, 2, 3, 0)
    got["w3_spline"] = np.ascontiguousarray(sw.reshape(P, 9, 9, C))
    sc = a["L3_conv_spline_scaler"].transpose(1, 2, 3, 0)
    got["w3_scaler"] = np.ascontiguousarray(np.broadcast_to(sc, (SPLINE,) + sc.shape).reshape(P, 9, 9, C))
    bw = a["L3_conv_base_weight"].transpose(3, 1, 2, 0)
    base = np.zeros((P, 2, 9, C), f32)
    base[:, 0] = bw[AROUND].reshape(P, 9, C)
    base[:C, 1] = bw[CENTER]
    got["w3_base"] = base
    got["w3_place"] = np.repeat(3.5 - np.arange(SPLINE), C).astype(f32).reshape(P, 1)
    bias = np.zeros((4, 32), f32)
    bias[:, :C] = a["L3_conv_bias_weight"]
    got["w3_bias"] = bias.reshape(P, 1)
    return got

def kernel(**inputs):
    import numpy as np
    import concourse.bacc as bacc
    from concourse.bass_utils import run_bass_kernel_spmd

    nc = bacc.Bacc("TRN2", target_bir_lowering=False, num_devices=1)
    arrays = lay_out(inputs)
    io = {k: nc.dram_tensor(f"in_{k}", v.shape, mybir.dt.from_np(v.dtype), kind="ExternalInput").ap() for k, v in arrays.items()}
    io["out"] = nc.dram_tensor("out_x", (NB, C, H, W), F32, kind="ExternalOutput").ap()
    build(nc, io)
    r = run_bass_kernel_spmd(nc, [{f"in_{k}": v for k, v in arrays.items()}], core_ids=[0])
    return r.results[0]["out_x"]
```
